# Optimizing a Trainium2 kernel written in Bass

```python
import numpy as np
import jax
import jax.numpy as jnp

def _softmax(x, axis=-1):
    return jax.nn.softmax(x, axis=axis)

def _gelu(x):
    return jax.nn.gelu(x, approximate=True)

def _silu(x):
    return jax.nn.silu(x)

def _sigmoid(x):
    return jax.nn.sigmoid(x)

def _layernorm(x, axis=-1, eps=1e-05):
    m = jnp.mean(x, axis=axis, keepdims=True)
    v = jnp.var(x, axis=axis, keepdims=True)
    return (x - m) / jnp.sqrt(v + eps)

def _scatter_add(tgt, idx, src, axis=0):
    return tgt.at[idx].add(src)

def _segment_sum(src, seg, n):
    return jax.ops.segment_sum(src, seg, n)
kernel_name = 'mk_vit_tower_postln_d2_tok_img256_r4_0cff98'

def setup_inputs(seed: int=0):
    np.random.seed(seed)
    _w = jnp.asarray

    def _rec_inputs():
        import jax
        import jax.numpy as jnp
        _rk = jax.random.key(seed)
        x = -0.000395706 + 0.999959 * jax.random.normal(jax.random.fold_in(_rk, 1), (64, 1, 96, 96), jnp.float32)
        return x
    x = _rec_inputs()

    def _L0_tok_setup():
        import jax, jax.numpy as jnp
        import numpy as np
        from jax import lax
        EMBED_DIM = 64
        key = jax.random.key(seed)
        ks = jax.random.split(key, 11)
        B, H, W = (64, 224, 224)
        D = EMBED_DIM
        x = jax.random.normal(ks[0], (B, 1, H, W), dtype=jnp.float32)
        conv_w = jax.random.normal(ks[1], (4, 1, 2, 2), dtype=jnp.float32) * 0.5
        conv_b = jax.random.normal(ks[2], (4,), dtype=jnp.float32) * 0.1
        s = 1.0 / np.sqrt(D)
        wq = jax.random.normal(ks[3], (D, D), dtype=jnp.float32) * s
        bq = jax.random.normal(ks[4], (D,), dtype=jnp.float32) * 0.02
        wk = jax.random.normal(ks[5], (D, D), dtype=jnp.float32) * s
        bk = jax.random.normal(ks[6], (D,), dtype=jnp.float32) * 0.02
        wv = jax.random.normal(ks[7], (D, D), dtype=jnp.float32) * s
        bv = jax.random.normal(ks[8], (D,), dtype=jnp.float32) * 0.02
        wo = jax.random.normal(ks[9], (D, D), dtype=jnp.float32) * s
        bo = jax.random.normal(ks[10], (D,), dtype=jnp.float32) * 0.02
        return {'x': x, 'conv_w': conv_w, 'conv_b': conv_b, 'wq': wq, 'bq': bq, 'wk': wk, 'bk': bk, 'wv': wv, 'bv': bv, 'wo': wo, 'bo': bo}
    _L0_tok_all = _L0_tok_setup()
    _L0_tok_in = {k: v for k, v in _L0_tok_all.items() if k in ('conv_w', 'conv_b', 'wq', 'bq', 'wk', 'bk', 'wv', 'bv', 'wo', 'bo')}
    del _L0_tok_all

    def _L0_attn_setup():
        import jax, jax.numpy as jnp
        import numpy as np
        SEQ_LEN = 512
        EMBED_DIM = 64
        BATCH = 8
        LN_EPS = 1e-05

        def _layernorm(x, g, b):
            mu = jnp.mean(x, axis=-1, keepdims=True)
            var = jnp.mean(jnp.square(x - mu), axis=-1, keepdims=True)
            return (x - mu) * jax.lax.rsqrt(var + LN_EPS) * g + b
        key = jax.random.key(seed)
        ks = jax.random.split(key, 8)
        C = EMBED_DIM
        x = jax.random.normal(ks[0], (BATCH, SEQ_LEN, C), dtype=jnp.float32)
        qkv_w = jax.random.normal(ks[1], (C, 3 * C), dtype=jnp.float32) * 0.02
        qkv_b = jnp.zeros((3 * C,), dtype=jnp.float32)
        proj_w = jax.random.normal(ks[2], (C, C), dtype=jnp.float32) * 0.02
        proj_b = jnp.zeros((C,), dtype=jnp.float32)
        ln1_g = jnp.ones((C,), dtype=jnp.float32)
        ln1_b = jnp.zeros((C,), dtype=jnp.float32)
        ln2_g = jnp.ones((C,), dtype=jnp.float32)
        ln2_b = jnp.zeros((C,), dtype=jnp.float32)
        bias_table = jax.random.truncated_normal(ks[3], -2.0, 2.0, (2 * SEQ_LEN - 1,), dtype=jnp.float32) * 0.02
        scale = jnp.asarray(1.0 / np.sqrt(C), dtype=jnp.float32)
        return {'x': x, 'ln1_g': ln1_g, 'ln1_b': ln1_b, 'qkv_w': qkv_w, 'qkv_b': qkv_b, 'bias_table': bias_table, 'scale': scale, 'proj_w': proj_w, 'proj_b': proj_b, 'ln2_g': ln2_g, 'ln2_b': ln2_b}
    _L0_attn_all = _L0_attn_setup()
    _L0_attn_in = {k: v for k, v in _L0_attn_all.items() if k in ('ln1_g', 'ln1_b', 'qkv_w', 'qkv_b', 'bias_table', 'scale', 'proj_w', 'proj_b', 'ln2_g', 'ln2_b')}
    del _L0_attn_all

    def _L0_ffn_setup():
        import jax, jax.numpy as jnp
        import numpy as np
        B, S, D = (8, 1024, 64)
        H = 4 * D
        CAPACITY = 0.5
        key = jax.random.key(seed)
        ks = jax.random.split(key, 6)
        x = jax.random.normal(ks[0], (B, S, D), dtype=jnp.float32)
        attention_mask = jnp.zeros((B, 1, 1, S), dtype=jnp.float32)
        wr = jax.random.normal(ks[1], (D, 1), dtype=jnp.float32) * 0.02
        br = jnp.zeros((1,), dtype=jnp.float32)
        w1 = jax.random.normal(ks[2], (D, H), dtype=jnp.float32) * 0.02
        b1 = jnp.zeros((H,), dtype=jnp.float32)
        w2 = jax.random.normal(ks[3], (H, D), dtype=jnp.float32) * 0.02
        b2 = jnp.zeros((D,), dtype=jnp.float32)
        return {'x': x, 'attention_mask': attention_mask, 'wr': wr, 'br': br, 'w1': w1, 'b1': b1, 'w2': w2, 'b2': b2}
    _L0_ffn_all = _L0_ffn_setup()
    _L0_ffn_in = {k: v for k, v in _L0_ffn_all.items() if k in ('attention_mask', 'wr', 'br', 'w1', 'b1', 'w2', 'b2')}
    del _L0_ffn_all

    def _L1_attn_setup():
        import jax, jax.numpy as jnp
        import numpy as np
        import math
        EMBED_DIM = 64
        SEQ_LEN = 1024
        BATCH = 4
        NUM_SCALES = (24.0, 720.0)
        key = jax.random.key(seed)
        ks = jax.random.split(key, 8)
        d = EMBED_DIM
        x = jax.random.normal(ks[0], (BATCH, SEQ_LEN, d), dtype=jnp.float32)
        s = 1.0 / math.sqrt(d)
        Wq = jax.random.uniform(ks[1], (d, d), jnp.float32, -s, s)
        bq = jax.random.uniform(ks[2], (d,), jnp.float32, -s, s)
        Wk = jax.random.uniform(ks[3], (d, d), jnp.float32, -s, s)
        bk = jax.random.uniform(ks[4], (d,), jnp.float32, -s, s)
        Wv = jax.random.uniform(ks[5], (d, d), jnp.float32, -s, s)
        bv = jax.random.uniform(ks[6], (d,), jnp.float32, -s, s)
        beta = jnp.ones((len(NUM_SCALES),), dtype=jnp.float32)
        return {'x': x, 'Wq': Wq, 'bq': bq, 'Wk': Wk, 'bk': bk, 'Wv': Wv, 'bv': bv, 'beta': beta}
    _L1_attn_all = _L1_attn_setup()
    _L1_attn_in = {k: v for k, v in _L1_attn_all.items() if k in ('Wq', 'bq', 'Wk', 'bk', 'Wv', 'bv', 'beta')}
    del _L1_attn_all

    def _L1_ffn_setup():
        import jax, jax.numpy as jnp
        import numpy as np
        B, K, D = (128, 16, 64)
        E = 32
        H = int(D * 0.25)
        key = jax.random.key(seed)
        ks = jax.random.split(key, 7)
        d_rs = D ** (-0.5)
        h_rs = H ** (-0.5)
        x = jax.random.normal(ks[0], (B, K, D), dtype=jnp.float32)
        router_w = jax.random.uniform(ks[1], (E, D), jnp.float32, -d_rs, d_rs)
        router_b = jax.random.uniform(ks[2], (E,), jnp.float32, -d_rs, d_rs)
        W1 = jax.random.uniform(ks[3], (E, D, H), jnp.float32, -h_rs, h_rs)
        b1 = jax.random.uniform(ks[4], (E, H), jnp.float32, -h_rs, h_rs)
        W2 = jax.random.uniform(ks[5], (E, H, D), jnp.float32, -d_rs, d_rs)
        b2 = jax.random.uniform(ks[6], (E, D), jnp.float32, -d_rs, d_rs)
        return {'x': x, 'router_w': router_w, 'router_b': router_b, 'W1': W1, 'b1': b1, 'W2': W2, 'b2': b2}
    _L1_ffn_all = _L1_ffn_setup()
    _L1_ffn_in = {k: v for k, v in _L1_ffn_all.items() if k in ('router_w', 'router_b', 'W1', 'b1', 'W2', 'b2')}
    del _L1_ffn_all
    return {'x': x, 'L0_tok_conv_w': _L0_tok_in['conv_w'], 'L0_tok_conv_b': _L0_tok_in['conv_b'], 'L0_tok_wq': _L0_tok_in['wq'], 'L0_tok_bq': _L0_tok_in['bq'], 'L0_tok_wk': _L0_tok_in['wk'], 'L0_tok_bk': _L0_tok_in['bk'], 'L0_tok_wv': _L0_tok_in['wv'], 'L0_tok_bv': _L0_tok_in['bv'], 'L0_tok_wo': _L0_tok_in['wo'], 'L0_tok_bo': _L0_tok_in['bo'], 'L0_attn_ln1_g': _L0_attn_in['ln1_g'], 'L0_attn_ln1_b': _L0_attn_in['ln1_b'], 'L0_attn_qkv_w': _L0_attn_in['qkv_w'], 'L0_attn_qkv_b': _L0_attn_in['qkv_b'], 'L0_attn_bias_table': _L0_attn_in['bias_table'], 'L0_attn_scale': _L0_attn_in['scale'], 'L0_attn_proj_w': _L0_attn_in['proj_w'], 'L0_attn_proj_b': _L0_attn_in['proj_b'], 'L0_attn_ln2_g': _L0_attn_in['ln2_g'], 'L0_attn_ln2_b': _L0_attn_in['ln2_b'], 'L0_ffn_attention_mask': _L0_ffn_in['attention_mask'], 'L0_ffn_wr': _L0_ffn_in['wr'], 'L0_ffn_br': _L0_ffn_in['br'], 'L0_ffn_w1': _L0_ffn_in['w1'], 'L0_ffn_b1': _L0_ffn_in['b1'], 'L0_ffn_w2': _L0_ffn_in['w2'], 'L0_ffn_b2': _L0_ffn_in['b2'], 'L1_attn_Wq': _L1_attn_in['Wq'], 'L1_attn_bq': _L1_attn_in['bq'], 'L1_attn_Wk': _L1_attn_in['Wk'], 'L1_attn_bk': _L1_attn_in['bk'], 'L1_attn_Wv': _L1_attn_in['Wv'], 'L1_attn_bv': _L1_attn_in['bv'], 'L1_attn_beta': _L1_attn_in['beta'], 'L1_ffn_router_w': _L1_ffn_in['router_w'], 'L1_ffn_router_b': _L1_ffn_in['router_b'], 'L1_ffn_W1': _L1_ffn_in['W1'], 'L1_ffn_b1': _L1_ffn_in['b1'], 'L1_ffn_W2': _L1_ffn_in['W2'], 'L1_ffn_b2': _L1_ffn_in['b2']}

def reference(x, L0_tok_conv_w, L0_tok_conv_b, L0_tok_wq, L0_tok_bq, L0_tok_wk, L0_tok_bk, L0_tok_wv, L0_tok_bv, L0_tok_wo, L0_tok_bo, L0_attn_ln1_g, L0_attn_ln1_b, L0_attn_qkv_w, L0_attn_qkv_b, L0_attn_bias_table, L0_attn_scale, L0_attn_proj_w, L0_attn_proj_b, L0_attn_ln2_g, L0_attn_ln2_b, L0_ffn_attention_mask, L0_ffn_wr, L0_ffn_br, L0_ffn_w1, L0_ffn_b1, L0_ffn_w2, L0_ffn_b2, L1_attn_Wq, L1_attn_bq, L1_attn_Wk, L1_attn_bk, L1_attn_Wv, L1_attn_bv, L1_attn_beta, L1_ffn_router_w, L1_ffn_router_b, L1_ffn_W1, L1_ffn_b1, L1_ffn_W2, L1_ffn_b2):
    import jax
    import jax.numpy as jnp

    def _L0_tok_ref(x, conv_w, conv_b, wq, bq, wk, bk, wv, bv, wo, bo):
        import jax, jax.numpy as jnp
        import numpy as np
        from jax import lax
        EMBED_DIM = 64
        B = x.shape[0]
        D = EMBED_DIM
        feat = lax.conv_general_dilated(x, conv_w, window_strides=(2, 2), padding='VALID', dimension_numbers=('NCHW', 'OIHW', 'NCHW'))
        feat = feat + conv_b[None, :, None, None]
        qfeat = feat.reshape(B, -1)
        seq_len = qfeat.shape[1] // D
        qfeat = qfeat.reshape(B, seq_len, D)
        Q = jnp.einsum('bsd,ed->bse', qfeat, wq) + bq
        K = jnp.einsum('bsd,ed->bse', qfeat, wk) + bk
        V = jnp.einsum('bsd,ed->bse', qfeat, wv) + bv
        scores = jax.nn.softmax(jnp.einsum('bse,bte->bst', Q, K) / jnp.sqrt(jnp.float32(D)), axis=-1)
        attn_out = jnp.einsum('bst,bte->bse', scores, V)
        out = jnp.einsum('bse,fe->bsf', attn_out, wo) + bo
        return out

    def _L0_attn_ref(x, ln1_g, ln1_b, qkv_w, qkv_b, bias_table, scale, proj_w, proj_b, ln2_g, ln2_b):
        import jax, jax.numpy as jnp
        import numpy as np
        SEQ_LEN = 512
        EMBED_DIM = 64
        BATCH = 8
        LN_EPS = 1e-05

        def _layernorm(x, g, b):
            mu = jnp.mean(x, axis=-1, keepdims=True)
            var = jnp.mean(jnp.square(x - mu), axis=-1, keepdims=True)
            return (x - mu) * jax.lax.rsqrt(var + LN_EPS) * g + b
        B, N, C = x.shape
        h = _layernorm(x, ln1_g, ln1_b)
        qkv = h @ qkv_w + qkv_b
        q, k, v = jnp.split(qkv, 3, axis=-1)
        coords = jnp.arange(N)
        rel_idx = coords[None, :] - coords[:, None] + (N - 1)
        rel_bias = bias_table[rel_idx]
        attn = jnp.einsum('bnc,bmc->bnm', q, k) + rel_bias
        attn = jax.nn.softmax(attn, axis=-1) * scale
        out = jnp.einsum('bnm,bmc->bnc', attn, v)
        out = out @ proj_w + proj_b
        out = _layernorm(out, ln2_g, ln2_b)
        return out

    def _L0_ffn_ref(x, attention_mask, wr, br, w1, b1, w2, b2):
        import jax, jax.numpy as jnp
        import numpy as np
        B, S, D = (8, 1024, 64)
        H = 4 * D
        CAPACITY = 0.5
        b, s, d = x.shape
        weights = (jnp.einsum('bsd,do->bso', x, wr) + br)[..., 0]
        k = max(1, int(CAPACITY * s))
        kk = k - 1 if k > 1 else 1
        _, idx = jax.lax.top_k(weights, k)
        sel_idx = idx[:, :kk]
        sel = jnp.take_along_axis(x, sel_idx[:, :, None], axis=1)
        h = jax.nn.gelu(jnp.einsum('bkd,dh->bkh', sel, w1) + b1)
        y = jnp.einsum('bkh,hd->bkd', h, w2) + b2
        w_sel = jnp.take_along_axis(weights, sel_idx, axis=1)
        y = y * w_sel[..., None]
        batch_idx = jnp.arange(b)[:, None]
        processed = jnp.zeros_like(x).at[batch_idx, sel_idx].set(y)
        return processed + x

    def _L1_attn_ref(x, Wq, bq, Wk, bk, Wv, bv, beta):
        import jax, jax.numpy as jnp
        import numpy as np
        import math
        EMBED_DIM = 64
        SEQ_LEN = 1024
        BATCH = 4
        NUM_SCALES = (24.0, 720.0)
        d = x.shape[-1]
        seq_len = x.shape[1]
        sqrt_d = jnp.asarray(math.sqrt(d), x.dtype)
        Q = jnp.einsum('bsd,ed->bse', x, Wq) + bq
        K = jnp.einsum('bsd,ed->bse', x, Wk) + bk
        V = jnp.einsum('bsd,ed->bse', x, Wv) + bv
        attn = jnp.einsum('bse,bte->bst', Q, K) / sqrt_d
        idx = jnp.arange(seq_len, dtype=jnp.float32)
        absdiff = jnp.abs(idx[:, None] - idx[None, :])
        two_pi = jnp.asarray(2.0 * math.pi, jnp.float32)
        bias = jnp.zeros((seq_len, seq_len), dtype=jnp.float32)
        for n, T in enumerate(NUM_SCALES):
            bias = bias + beta[n] * jnp.cos(two_pi * absdiff / T)
        scores = jax.nn.softmax(attn + bias[None, :, :], axis=-1)
        return jnp.einsum('bst,bte->bse', scores, V)

    def _L1_ffn_ref(x, router_w, router_b, W1, b1, W2, b2):
        import jax, jax.numpy as jnp
        import numpy as np
        B, K, D = (128, 16, 64)
        E = 32
        H = int(D * 0.25)
        xf = x.reshape(-1, D)
        logits = xf @ router_w.T + router_b
        idx = jnp.argmax(logits, axis=-1)
        w1t = jnp.take(W1, idx, axis=0)
        h = jnp.einsum('nd,ndh->nh', xf, w1t) + jnp.take(b1, idx, axis=0)
        h = jax.nn.relu(h)
        w2t = jnp.take(W2, idx, axis=0)
        out = jnp.einsum('nh,nhd->nd', h, w2t) + jnp.take(b2, idx, axis=0)
        out = jax.nn.relu(out)
        return out.reshape(x.shape)
    h = _L0_tok_ref(x, L0_tok_conv_w, L0_tok_conv_b, L0_tok_wq, L0_tok_bq, L0_tok_wk, L0_tok_bk, L0_tok_wv, L0_tok_bv, L0_tok_wo, L0_tok_bo)
    h = _layernorm(h + _L0_attn_ref(h, L0_attn_ln1_g, L0_attn_ln1_b, L0_attn_qkv_w, L0_attn_qkv_b, L0_attn_bias_table, L0_attn_scale, L0_attn_proj_w, L0_attn_proj_b, L0_attn_ln2_g, L0_attn_ln2_b), axis=-1)
    h = _layernorm(h + _L0_ffn_ref(h, L0_ffn_attention_mask, L0_ffn_wr, L0_ffn_br, L0_ffn_w1, L0_ffn_b1, L0_ffn_w2, L0_ffn_b2), axis=-1)
    h = _layernorm(h + _L1_attn_ref(h, L1_attn_Wq, L1_attn_bq, L1_attn_Wk, L1_attn_bk, L1_attn_Wv, L1_attn_bv, L1_attn_beta), axis=-1)
    h = _layernorm(h + _L1_ffn_ref(h, L1_ffn_router_w, L1_ffn_router_b, L1_ffn_W1, L1_ffn_b1, L1_ffn_W2, L1_ffn_b2), axis=-1)
    return h

_drawn_inputs = setup_inputs


def setup_inputs(seed=0):
    import zlib

    import numpy as np

    out = dict(_drawn_inputs(seed))
    spreads = {'L0_attn_ln1_g': (1.0, 0.6),
     'L0_attn_ln1_b': (0.0, 0.8),
     'L0_attn_qkv_b': (0.0, 0.333),
     'L0_attn_proj_b': (0.0, 0.1),
     'L0_attn_ln2_g': (1.0, 0.2),
     'L0_attn_ln2_b': (0.0, 0.1),
     'L0_ffn_b1': (0.0, 0.8),
     'L0_ffn_b2': (0.0, 0.701),
     'L1_attn_beta': (1.0, 0.6)}
    factors = {'L0_tok_bq': 6.589,
     'L0_tok_bk': 8.0,
     'L0_tok_bv': 2.747,
     'L0_attn_qkv_w': 3.392,
     'L0_attn_bias_table': 8.0,
     'L0_ffn_wr': 5.294,
     'L0_ffn_w1': 8.0,
     'L0_ffn_w2': 8.0,
     'L1_attn_Wq': 5.347,
     'L1_attn_bq': 8.0,
     'L1_attn_Wk': 5.621,
     'L1_attn_bk': 8.0,
     'L1_ffn_b1': 3.776}
    for name, (base, spread) in spreads.items():
        noise = np.random.default_rng([zlib.crc32(name.encode()), seed]).standard_normal(out[name].shape)
        drawn = base * np.exp(spread * noise) if base else spread * noise
        out[name] = jnp.asarray(drawn.astype(out[name].dtype))
    for name, factor in factors.items():
        out[name] = (out[name] * factor).astype(out[name].dtype)
    return out
```

```python
from contextlib import ExitStack

import concourse.bass as bass
from concourse import mybir
import numpy as np

F32 = mybir.dt.float32
ALU = mybir.AluOpType
ACT = mybir.ActivationFunctionType
AX_X = mybir.AxisListType.X

IMAGES, TOKENS, FEAT = 64, 144, 64
HALF = TOKENS // 2
GROUP = 8
ITERS = IMAGES // GROUP
PAIRS = GROUP // 2
PAIR_TOKENS = 2 * TOKENS
CHANNELS = 4
PER_CHANNEL = TOKENS // CHANNELS
ONE = FEAT
AUG = FEAT + 1
SCALES = (24.0, 720.0)
AUGC = AUG + 2 * len(SCALES)
EXPERTS, HIDDEN = 32, 16
MOE_H = EXPERTS * HIDDEN
CAT = FEAT + EXPERTS
FFN_H = 4 * FEAT
TOPK = TOKENS // 2 - 1
OFF = -1.0e30
LOWEST = -3.4028234663852886e38
EPS = 1e-5

SECTIONS = dict(
    ident=(128, 128), eye2=(128, FEAT), convw=(128, 2 * CHANNELS), convb=(FEAT, CHANNELS), xinit=(AUGC, TOKENS),
    wqA=(FEAT, AUG), wkA=(FEAT, AUG), wvA=(FEAT, AUG), woA=(FEAT, FEAT), vaddA=(AUG, AUG),
    wqB=(FEAT, FEAT), wkB=(FEAT, FEAT), wvB=(FEAT, FEAT), qkvb=(FEAT, 3), g1=(FEAT, FEAT), b1=(FEAT, FEAT),
    projB=(FEAT, FEAT), scaleB=(128, 1), vaddB=(AUG, AUG), g2=(HALF, FEAT), b2=(HALF, FEAT),
    bias=(HALF, PAIR_TOKENS),
    wr=(AUG, 1), w1=(AUG, FFN_H), w2=(128, 2 * FEAT), fb2=(HALF, FEAT),
    wqD=(FEAT, AUGC), wkD=(FEAT, AUGC), betaD=(AUGC, AUGC), vD=(AUG, AUG),
    router=(AUG, EXPERTS), ew1=(CAT, MOE_H), ew2=(128, 4 * FEAT), eb2=(CAT, FEAT), desc=(HALF, EXPERTS),
)
START = {}
_at = 0
for _name, (_rows, _cols) in SECTIONS.items():
    START[_name] = _at
    _at += _cols
PARAM_COLS = _at


class Step:

    def __init__(self, sem, per, head):
        self.sem, self.per, self.head = sem, per, head

    def count(self, it, n):
        return it * self.per + (n + self.head)


def build(nc, pixels, params, out):
    with ExitStack() as ctx:
        def sb(name, shape):
            return ctx.enter_context(nc.sbuf_tensor(name, shape, F32))

        def psum(name):
            return ctx.enter_context(nc.psum_tensor(name, [128, 512], F32))

        def step(name, per, head=0):
            return Step(ctx.enter_context(nc.semaphore(name)), per, head)

        par = sb("par", [128, PARAM_COLS])

        def P(name, c0=0, c1=None):
            rows, cols = SECTIONS[name]
            return par[0:rows, START[name] + c0:START[name] + (cols if c1 is None else c1)]

        conv_lhs = sb("conv_lhs", [128, CHANNELS, 2, FEAT])
        a_mat = [sb("a_mat0", [AUG, AUG]), sb("a_mat1", [AUG, AUG]), sb("a_mat2", [AUGC, AUGC])]
        v_mat = [sb("v_mat0", [AUG, AUG]), sb("v_mat1", [AUG, AUG]), None]
        qkv_fold = sb("qkv_fold", [FEAT, 3, AUG])
        qkv_sum = sb("qkv_sum", [FEAT, 3])
        fold_tmp = sb("fold_tmp", [FEAT, 3, FEAT])
        neg_half = sb("neg_half", [HALF, 4])

        pix = sb("pix", [128, 2, GROUP, PER_CHANNEL])
        featT = sb("featT", [AUG, GROUP, TOKENS])
        xT = sb("xT", [AUGC, GROUP, TOKENS])
        gT = sb("gT", [AUGC, 2, PAIR_TOKENS])
        val = sb("val", [HALF, 4, 4, AUG])
        prob = sb("prob", [HALF, 4, 2, TOKENS])
        probT = sb("probT", [HALF, 2, 2, TOKENS])
        peak = sb("peak", [HALF, 4, 2])
        rsum = sb("rsum", [HALF, 4, 4])
        att = sb("att", [HALF, 4, 4, FEAT])
        h1 = sb("h1", [HALF, 4, 4, FEAT])
        h2 = sb("h2", [HALF, 4, 4, FEAT])
        h3 = sb("h3", [HALF, 4, 4, FEAT])
        xn = sb("xn", [HALF, 4, 4, FEAT])
        on = sb("on", [HALF, 4, 4, FEAT])
        y = sb("y", [HALF, 4, 4, FEAT])
        u = sb("u", [HALF, 4, 4, FEAT])
        cen = sb("cen", [HALF, 4, 4, FEAT])
        sq = sb("sq", [HALF, 4, 4, FEAT])
        mean = sb("mean", [HALF, 4, 4])
        var = sb("var", [HALF, 4, 4])
        rstd = sb("rstd", [HALF, 4, 4])
        resid = sb("resid", [HALF, 4, 4, FEAT])
        res = sb("res", [HALF, 4, 4, FEAT])
        cat = sb("cat", [HALF, 4, 4, CAT])
        hid = sb("hid", [128, 2, 2, PAIR_TOKENS])
        wcol = sb("wcol", [HALF, 2, GROUP])
        wrow = sb("wrow", [GROUP, TOKENS])
        work = sb("work", [GROUP, TOKENS])
        top8 = sb("top8", [GROUP, 8])
        wmrow = sb("wmrow", [GROUP, TOKENS])
        wm = sb("wm", [HALF, 2, GROUP])
        lmax = sb("lmax", [HALF, 4, 2, 4])
        hit = sb("hit", [HALF, 4, 4, EXPERTS])
        rank = sb("rank", [HALF, 4, 4, EXPERTS])
        catT = sb("catT", [CAT, 3, PAIR_TOKENS])
        ehid = sb("ehid", [128, 2, 4, PAIR_TOKENS])

        big = [psum(f"big{i}") for i in range(4)]
        bank_g, bank_v, bank_o, bank_x = psum("bank_g"), psum("bank_v"), psum("bank_o"), psum("bank_x")

        L = 3
        params_in = step("params_in", 0)
        folded_dve = step("folded_dve", 0)
        folded_pe = step("folded_pe", 0)
        setup_done = step("setup_done", 0)
        pixels_in = step("pixels_in", 16)
        conv_ready = step("conv_ready", CHANNELS)
        feat_ready = step("feat_ready", CHANNELS)
        turned = step("turned", 4 * PAIRS)
        x_ready = step("x_ready", 4 * PAIRS, head=1)
        g_ready = step("g_ready", L * PAIRS)
        g_copied = step("g_copied", L * PAIRS, head=1)
        v_ready = step("v_ready", L * PAIRS)
        v_copied = step("v_copied", L * PAIRS, head=1)
        scores_ready = step("scores_ready", L * GROUP)
        biased = step("biased", GROUP)
        peaked = step("peaked", L * GROUP)
        shifted = step("shifted", L * GROUP)
        exp_done = step("exp_done", L * GROUP)
        probs_turned = step("probs_turned", L * GROUP)
        probT_ready = step("probT_ready", L * GROUP)
        out_ready = step("out_ready", 5 * PAIRS)
        bank_o_read = step("bank_o_read", 5 * PAIRS, head=1)
        sum_inverted = step("sum_inverted", L * PAIRS)
        att_ready = step("att_ready", PAIRS)
        u_ready = step("u_ready", PAIRS)
        N_NORM = 6
        summed = step("summed", N_NORM * PAIRS)
        centred = step("centred", N_NORM * PAIRS)
        squared = step("squared", N_NORM * PAIRS)
        var_ready = step("var_ready", N_NORM * PAIRS)
        var_eps = step("var_eps", N_NORM * PAIRS)
        rstd_ready = step("rstd_ready", N_NORM * PAIRS)
        normed = step("normed", N_NORM * PAIRS)
        gained = step("gained", 2 * PAIRS)
        res_ready = step("res_ready", PAIRS)
        w_ready = step("w_ready", 1)
        w_copied = step("w_copied", 1)
        w_turned = step("w_turned", 1)
        top_step = step("top_step", 22)
        wm_turned = step("wm_turned", 1)
        wm_ready = step("wm_ready", 1)
        hid_ready = step("hid_ready", 2 * PAIRS)
        gelu_done = step("gelu_done", 2 * PAIRS)
        y_scaled = step("y_scaled", 2 * PAIRS)
        logits_ready = step("logits_ready", PAIRS)
        route = step("route", 4 * PAIRS)
        routed = step("routed", PAIRS)
        cat_turned = step("cat_turned", PAIRS)
        catT_ready = step("catT_ready", PAIRS, head=1)
        ehid_ready = step("ehid_ready", 4 * PAIRS)
        relu_act = step("relu_act", 2 * PAIRS)
        relu_dve = step("relu_dve", 2 * PAIRS)
        stored = [step(f"stored{j}", 16, head=16) for j in range(PAIRS)]

        pe_gate = step("pe_gate", 0)
        dve_gate = step("dve_gate", 0)
        pool_gate = step("pool_gate", 0)

        def hold(eng, gate):
            eng.sem_inc(gate.sem, 1)

        block = ctx.enter_context(nc.Block())

        def bc(ap2, n):
            return ap2.unsqueeze(2).to_broadcast([ap2.shape[0], ap2.shape[1], n])

        def row(ap2, n):
            return ap2.unsqueeze(1).to_broadcast([ap2.shape[0], n, ap2.shape[1]])

        LN_IN, LN_ATT, LN_B, LN_FFN, LN_D, LN_MOE = range(N_NORM)
        O_ATT = (0, 1, 3)
        O_FFN, O_MOE = 2, 4

        @block.sync
        def _(sp):
            sp.dma_start(par[:, :], params[:, :]).then_inc(params_in.sem, 16)
            sp.dma_start(pix[:, :, :, :], pixels[:, :, 0:GROUP, :]).then_inc(pixels_in.sem, 16)

            def store(it):
                for j in range(PAIRS):
                    sp.wait_ge(normed.sem, normed.count(it, LN_MOE * PAIRS + j + 1))
                    dst = out[bass.ds(it * GROUP + 2 * j, 2), :, :].rearrange("b (h p) d -> p (b h) d", p=HALF)
                    sp.dma_start(dst, res[:, j, :, :]).then_inc(stored[j].sem, 16)

            with sp.Fori(0, ITERS - 1) as it:
                sp.wait_ge(conv_ready.sem, conv_ready.count(it, CHANNELS))
                sp.dma_start(pix[:, :, :, :], pixels[:, :, bass.ds((it + 1) * GROUP, GROUP), :]).then_inc(pixels_in.sem, 16)
                store(it)
            store(ITERS - 1)
            for j in range(PAIRS):
                sp.wait_ge(stored[j].sem, 16 * (ITERS + 1))

        @block.tensor
        def _(pe):
            for head_start in (x_ready, g_copied, v_copied, bank_o_read, catT_ready):
                pe.sem_inc(head_start.sem, head_start.head)
            pe.wait_ge(params_in.sem, 16)
            pe.matmul(bank_g[0:AUG, 0:AUG], P("wqA"), P("wkA"), start=True, stop=True)
            pe.matmul(bank_g[0:AUGC, 128:128 + AUGC], P("wqD"), P("wkD"), start=True, stop=True)
            pe.matmul(bank_v[0:AUG, 0:FEAT], P("wvA"), P("woA"), start=True, stop=True).then_inc(folded_pe.sem, 1)
            pe.wait_ge(folded_dve.sem, 3)
            pe.matmul(bank_o[0:AUG, 0:AUG], qkv_fold[:, 0, :], qkv_fold[:, 1, :], start=True, stop=True)
            pe.matmul(bank_x[0:AUG, 0:FEAT], qkv_fold[:, 2, :], P("projB"), start=True, stop=True).then_inc(folded_pe.sem, 1)
            pe.wait_ge(setup_done.sem, 1)

            def conv(it):
                pe.wait_ge(pixels_in.sem, pixels_in.count(it, 16))
                for c in range(CHANNELS):
                    for a in range(2):
                        mm = pe.matmul(big[c][0:FEAT, 0:GROUP * PER_CHANNEL], conv_lhs[:, c, a, :],
                                       pix[:, a, :, :], start=a == 0, stop=a == 1)
                    mm.then_inc(conv_ready.sem, 1)

            def turn(it, stage, j):
                n = stage * PAIRS + j
                ln = (LN_IN, LN_B, LN_FFN, LN_D)[stage]
                src = (xn[:, j, :, :], h2[:, j, :, :], h3[:, j, :, :], cat[:, j, :, 0:FEAT])[stage]
                pe.wait_ge(normed.sem, normed.count(it, ln * PAIRS + j + 1))
                pe.wait_ge(x_ready.sem, x_ready.count(it, n))
                hold(pe, pe_gate)
                for t in range(4):
                    mm = pe.transpose(bank_x[0:FEAT, t * HALF:(t + 1) * HALF], src[:, t, :], P("ident")[0:HALF, 0:HALF])
                mm.then_inc(turned.sem, 1)

            def attention(it, layer):
                rows = AUGC if layer == 2 else AUG
                src = featT if layer == 0 else xT
                vw = P("vD") if layer == 2 else v_mat[layer][:, :]

                def project(j):
                    if layer == 0:
                        pe.wait_ge(feat_ready.sem, feat_ready.count(it, CHANNELS))
                    else:
                        pe.wait_ge(x_ready.sem, x_ready.count(it, (2 * layer - 2) * PAIRS + j + 1))
                    n = layer * PAIRS + j
                    pe.wait_ge(g_copied.sem, g_copied.count(it, n))
                    pe.matmul(bank_g[0:rows, 0:PAIR_TOKENS], a_mat[layer][:, :],
                              src[0:rows, 2 * j:2 * j + 2, :], start=True, stop=True).then_inc(g_ready.sem, 1)
                    pe.wait_ge(v_copied.sem, v_copied.count(it, n))
                    for t in range(4):
                        mm = pe.matmul(bank_v[0:HALF, t * AUG:(t + 1) * AUG],
                                       src[0:AUG, 2 * j + t // 2, (t % 2) * HALF:(t % 2 + 1) * HALF], vw,
                                       start=True, stop=True)
                    mm.then_inc(v_ready.sem, 1)

                def scores(k):
                    n = layer * GROUP + k
                    pe.wait_ge(g_copied.sem, g_copied.count(it, layer * PAIRS + k // 2 + 1))
                    if k >= 2:
                        if layer == 1:
                            pe.wait_ge(biased.sem, biased.count(it, k - 1))
                        else:
                            pe.wait_ge(shifted.sem, shifted.count(it, n - 1))
                    for h in range(2):
                        c = (k % 2) * TOKENS + h * HALF
                        mm = pe.matmul(big[k % 2][0:HALF, h * TOKENS:(h + 1) * TOKENS],
                                       gT[0:rows, (k // 2) % 2, c:c + HALF], src[0:rows, k, :], start=True, stop=True)
                    mm.then_inc(scores_ready.sem, 1)

                def turn_probs(k):
                    n = layer * GROUP + k
                    pe.wait_ge(exp_done.sem, exp_done.count(it, n + 1))
                    if k >= 2:
                        pe.wait_ge(probT_ready.sem, probT_ready.count(it, n - 1))
                    for th in range(2):
                        for sh in range(2):
                            c = th * TOKENS + sh * HALF
                            mm = pe.transpose(big[2 + k % 2][0:HALF, c:c + HALF],
                                              prob[:, k % 4, sh, th * HALF:(th + 1) * HALF], P("ident")[0:HALF, 0:HALF])
                    mm.then_inc(probs_turned.sem, 1)

                def weigh(k):
                    j = k // 2
                    pe.wait_ge(probT_ready.sem, probT_ready.count(it, layer * GROUP + k + 1))
                    pe.wait_ge(v_copied.sem, v_copied.count(it, layer * PAIRS + j + 1))
                    if k % 2 == 0:
                        pe.wait_ge(bank_o_read.sem, bank_o_read.count(it, O_ATT[layer] * PAIRS + j))
                    for sh in range(2):
                        t = (k % 2) * 2 + sh
                        for th in range(2):
                            mm = pe.matmul(bank_o[0:HALF, t * AUG:(t + 1) * AUG],
                                           probT[:, k % 2, th, sh * HALF:(sh + 1) * HALF],
                                           val[:, j, (k % 2) * 2 + th, :], start=th == 0, stop=th == 1)
                    if k % 2 == 1:
                        mm.then_inc(out_ready.sem, 1)

                for i in range(GROUP + 5):
                    if 0 <= i - 2 < GROUP:
                        scores(i - 2)
                    if i % 2 == 0 and i // 2 < PAIRS and layer > 0:
                        turn(it, 2 * layer - 2, i // 2)
                    if i % 2 == 1 and i // 2 < PAIRS:
                        project(i // 2)
                    if 0 <= i - 5 < GROUP:
                        weigh(i - 5)
                    if 0 <= i - 4 < GROUP:
                        turn_probs(i - 4)

            def ffn(it):
                for j in range(PAIRS):
                    turn(it, 1, j)
                    pe.wait_ge(x_ready.sem, x_ready.count(it, PAIRS + j + 1))
                    for t in range(4):
                        col = (t % 2) * GROUP + 2 * j + t // 2
                        mm = pe.matmul(bank_g[0:HALF, col:col + 1],
                                       xT[0:AUG, 2 * j + t // 2, (t % 2) * HALF:(t % 2 + 1) * HALF], P("wr"),
                                       start=True, stop=True)
                mm.then_inc(w_ready.sem, 1)

                def hidden(j):
                    for c in range(2):
                        n = 2 * j + c
                        if n >= 4:
                            pe.wait_ge(gelu_done.sem, gelu_done.count(it, n - 3))
                        pe.matmul(big[n % 4][:, 0:PAIR_TOKENS], P("w1", 128 * c, 128 * (c + 1)),
                                  xT[0:AUG, 2 * j:2 * j + 2, :], start=True, stop=True).then_inc(hid_ready.sem, 1)

                def second(j):
                    pe.wait_ge(gelu_done.sem, gelu_done.count(it, 2 * j + 2))
                    pe.wait_ge(bank_o_read.sem, bank_o_read.count(it, O_FFN * PAIRS + j))
                    for t in range(4):
                        for c in range(2):
                            mm = pe.matmul(bank_o[0:HALF, t * FEAT:(t + 1) * FEAT],
                                           hid[:, j % 2, c, t * HALF:(t + 1) * HALF], P("w2", c * FEAT, (c + 1) * FEAT),
                                           start=c == 0, stop=c == 1)
                    mm.then_inc(out_ready.sem, 1)

                hidden(0)
                pe.wait_ge(w_copied.sem, w_copied.count(it, 1))
                for h in range(2):
                    mm = pe.transpose(bank_v[0:GROUP, h * HALF:(h + 1) * HALF], wcol[:, h, :], P("ident")[0:HALF, 0:HALF])
                mm.then_inc(w_turned.sem, 1)
                for j in range(1, PAIRS):
                    hidden(j)
                    second(j - 1)
                second(PAIRS - 1)
                pe.wait_ge(top_step.sem, top_step.count(it, 22))
                hold(pe, pe_gate)
                for h in range(2):
                    mm = pe.transpose(bank_g[0:HALF, 64 + h * GROUP:64 + (h + 1) * GROUP],
                                      wmrow[:, h * HALF:(h + 1) * HALF], P("ident")[0:GROUP, 0:GROUP])
                mm.then_inc(wm_turned.sem, 1)

            def moe(it):
                def logits(j):
                    pe.wait_ge(x_ready.sem, x_ready.count(it, 3 * PAIRS + j + 1))
                    if j >= 1:
                        pe.wait_ge(route.sem, route.count(it, 4 * j - 2))
                    for t in range(4):
                        mm = pe.matmul(bank_g[0:HALF, t * EXPERTS:(t + 1) * EXPERTS],
                                       xT[0:AUG, 2 * j + t // 2, (t % 2) * HALF:(t % 2 + 1) * HALF], P("router"),
                                       start=True, stop=True)
                    mm.then_inc(logits_ready.sem, 1)

                def turn_cat(j):
                    pe.wait_ge(routed.sem, routed.count(it, j + 1))
                    pe.wait_ge(catT_ready.sem, catT_ready.count(it, j))
                    for t in range(4):
                        mm = pe.transpose(bank_v[0:CAT, t * HALF:(t + 1) * HALF], cat[:, j, t, :],
                                          P("ident")[0:HALF, 0:HALF])
                    mm.then_inc(cat_turned.sem, 1)

                def hidden(j):
                    pe.wait_ge(catT_ready.sem, catT_ready.count(it, j + 1))
                    for c in range(4):
                        if j >= 1:
                            done = relu_dve if c % 2 else relu_act
                            pe.wait_ge(done.sem, done.count(it, 2 * (j - 1) + c // 2 + 1))
                        pe.matmul(big[c][:, 0:PAIR_TOKENS], P("ew1", 128 * c, 128 * (c + 1)),
                                  catT[:, j % 3, :], start=True, stop=True).then_inc(ehid_ready.sem, 1)

                def second(j):
                    pe.wait_ge(relu_act.sem, relu_act.count(it, 2 * j + 2))
                    pe.wait_ge(relu_dve.sem, relu_dve.count(it, 2 * j + 2))
                    pe.wait_ge(bank_o_read.sem, bank_o_read.count(it, O_MOE * PAIRS + j))
                    for t in range(4):
                        for c in range(4):
                            pe.matmul(bank_o[0:HALF, t * FEAT:(t + 1) * FEAT],
                                      ehid[:, j % 2, c, t * HALF:(t + 1) * HALF], P("ew2", c * FEAT, (c + 1) * FEAT),
                                      start=c == 0, stop=False)
                        mm = pe.matmul(bank_o[0:HALF, t * FEAT:(t + 1) * FEAT],
                                       catT[FEAT:CAT, j % 3, t * HALF:(t + 1) * HALF], P("eb2")[FEAT:CAT, :],
                                       start=False, stop=True)
                    mm.then_inc(out_ready.sem, 1)

                for i in range(PAIRS + 4):
                    if 0 <= i - 4 < PAIRS:
                        second(i - 4)
                    if i < PAIRS:
                        turn(it, 3, i)
                    if 0 <= i - 1 < PAIRS:
                        logits(i - 1)
                    if 0 <= i - 2 < PAIRS:
                        turn_cat(i - 2)
                    if 0 <= i - 3 < PAIRS:
                        hidden(i - 3)

            with pe.Fori(0, ITERS) as it:
                conv(it)
                attention(it, 0)
                attention(it, 1)
                ffn(it)
                attention(it, 2)
                moe(it)

        @block.scalar
        def _(act):
            def conv_out(it):
                for c in range(CHANNELS):
                    act.wait_ge(conv_ready.sem, conv_ready.count(it, c + 1))
                    act.activation(featT[0:FEAT, :, c * PER_CHANNEL:(c + 1) * PER_CHANNEL],
                                   big[c][0:FEAT, 0:GROUP * PER_CHANNEL].rearrange("p (b j) -> p b j", b=GROUP),
                                   ACT.Identity, bias=P("convb", c, c + 1)).then_inc(feat_ready.sem, 1)

            def copy_x(it, stage, j):
                act.wait_ge(turned.sem, turned.count(it, stage * PAIRS + j + 1))
                act.copy(xT[0:FEAT, 2 * j:2 * j + 2, :],
                         bank_x[0:FEAT, 0:PAIR_TOKENS].rearrange("p (b s) -> p b s", b=2)).then_inc(x_ready.sem, 1)

            def attention(it, layer):
                rows = AUGC if layer == 2 else AUG

                def copy_projected(j):
                    act.wait_ge(g_ready.sem, g_ready.count(it, layer * PAIRS + j + 1))
                    act.copy(gT[0:rows, j % 2, :], bank_g[0:rows, 0:PAIR_TOKENS]).then_inc(g_copied.sem, 1)
                    act.wait_ge(v_ready.sem, v_ready.count(it, layer * PAIRS + j + 1))
                    act.copy(val[:, j, :, :], bank_v[0:HALF, 0:4 * AUG].rearrange("p (t e) -> p t e", t=4))\
                       .then_inc(v_copied.sem, 1)

                def exponent(k):
                    act.wait_ge(shifted.sem, shifted.count(it, layer * GROUP + k + 1))
                    act.activation(prob[:, k % 4, :, :], prob[:, k % 4, :, :], ACT.Exp).then_inc(exp_done.sem, 1)

                def copy_probs(k):
                    act.wait_ge(probs_turned.sem, probs_turned.count(it, layer * GROUP + k + 1))
                    act.copy(probT[:, k % 2, :, :],
                             big[2 + k % 2][0:HALF, 0:PAIR_TOKENS].rearrange("p (h s) -> p h s", h=2))\
                       .then_inc(probT_ready.sem, 1)

                for i in range(GROUP + 5):
                    if i % 2 == 0 and i // 2 < PAIRS and layer > 0:
                        copy_x(it, 2 * layer - 2, i // 2)
                    if i % 2 == 1 and i // 2 < PAIRS:
                        copy_projected(i // 2)
                    if 0 <= i - 4 < GROUP:
                        copy_probs(i - 4)
                    if 0 <= i - 3 < GROUP:
                        exponent(i - 3)

            def ffn(it):
                for j in range(PAIRS):
                    copy_x(it, 1, j)

                def gelu(j):
                    for c in range(2):
                        n = 2 * j + c
                        act.wait_ge(hid_ready.sem, hid_ready.count(it, n + 1))
                        if j >= 2 and c == 0:
                            act.wait_ge(out_ready.sem, out_ready.count(it, O_FFN * PAIRS + j - 1))
                        act.activation(hid[:, j % 2, c, :], big[n % 4][:, 0:PAIR_TOKENS], ACT.Gelu_apprx_tanh)\
                           .then_inc(gelu_done.sem, 1)

                def copy_y(j):
                    act.wait_ge(out_ready.sem, out_ready.count(it, O_FFN * PAIRS + j + 1))
                    act.copy(y[:, j, :, :], bank_o[0:HALF, 0:4 * FEAT].rearrange("p (t e) -> p t e", t=4))\
                       .then_inc(bank_o_read.sem, 1)

                gelu(0)
                for j in range(1, PAIRS):
                    gelu(j)
                    copy_y(j - 1)
                copy_y(PAIRS - 1)

            def moe(it):
                def copy_cat(j):
                    act.wait_ge(cat_turned.sem, cat_turned.count(it, j + 1))
                    act.copy(catT[:, j % 3, :], bank_v[0:CAT, 0:PAIR_TOKENS]).then_inc(catT_ready.sem, 1)

                def relu(j):
                    for c in (0, 2):
                        act.wait_ge(ehid_ready.sem, ehid_ready.count(it, 4 * j + c + 1))
                        act.activation(ehid[:, j % 2, c, :], big[c][:, 0:PAIR_TOKENS], ACT.Relu).then_inc(relu_act.sem, 1)

                for i in range(PAIRS + 4):
                    if i < PAIRS:
                        copy_x(it, 3, i)
                    if 0 <= i - 2 < PAIRS:
                        copy_cat(i - 2)
                    if 0 <= i - 3 < PAIRS:
                        relu(i - 3)

            act.wait_ge(params_in.sem, 16)
            with act.Fori(0, ITERS) as it:
                conv_out(it)
                attention(it, 0)
                attention(it, 1)
                ffn(it)
                attention(it, 2)
                moe(it)

        @block.vector
        def _(dve):
            dve.memset(neg_half[:, :], -0.5)
            dve.wait_ge(params_in.sem, 16)
            qkv_cols = par[0:FEAT, START["wqB"]:START["wqB"] + 3 * FEAT].rearrange("p (n c) -> p n c", n=3)
            dve.tensor_tensor(fold_tmp[:, :, :], qkv_cols, row(P("b1"), 3), ALU.mult).then_inc(folded_dve.sem, 1)
            dve.wait_ge(folded_dve.sem, 1)
            dve.tensor_reduce(qkv_sum[:, :], fold_tmp[:, :, :], AX_X, ALU.add).then_inc(folded_dve.sem, 1)
            dve.wait_ge(folded_dve.sem, 2)
            dve.tensor_tensor(qkv_fold[:, :, 0:FEAT], qkv_cols, row(P("g1"), 3), ALU.mult)
            dve.tensor_tensor(qkv_fold[:, :, FEAT:AUG], qkv_sum[:, :].unsqueeze(2), P("qkvb").unsqueeze(2), ALU.add)\
               .then_inc(folded_dve.sem, 1)
            for c in range(CHANNELS):
                for a in range(2):
                    dve.tensor_scalar(conv_lhs[:, c, a, :], P("eye2"), P("convw", 2 * c + a, 2 * c + a + 1), None, ALU.mult)
            dve.tensor_copy(featT[0:AUG, :, :], row(P("xinit")[0:AUG, :], GROUP))
            dve.tensor_copy(xT[:, :, :], row(P("xinit"), GROUP))
            root = 1.0 / float(FEAT) ** 0.5
            dve.wait_ge(folded_pe.sem, 1)
            dve.tensor_scalar(a_mat[0][:, :], bank_g[0:AUG, 0:AUG], root, None, ALU.mult)
            dve.scalar_tensor_tensor(a_mat[2][:, :], bank_g[0:AUGC, 128:128 + AUGC], root, P("betaD"), ALU.mult, ALU.add)
            dve.tensor_copy(v_mat[0][:, FEAT:AUG], P("vaddA", FEAT, AUG))
            dve.tensor_tensor(v_mat[0][:, 0:FEAT], bank_v[0:AUG, 0:FEAT], P("vaddA", 0, FEAT), ALU.add)
            dve.wait_ge(folded_pe.sem, 2)
            dve.tensor_copy(a_mat[1][:, :], bank_o[0:AUG, 0:AUG])
            dve.tensor_copy(v_mat[1][:, FEAT:AUG], P("vaddB", FEAT, AUG))
            dve.scalar_tensor_tensor(v_mat[1][:, 0:FEAT], bank_x[0:AUG, 0:FEAT], P("scaleB")[0:AUG, :],
                                     P("vaddB", 0, FEAT), ALU.mult, ALU.add).then_inc(setup_done.sem, 1)

            def centre(it, ln, j, src, ready, need):
                n = ln * PAIRS + j
                dve.wait_ge(ready.sem, need)
                dve.tensor_reduce(mean[:, j, :], src, AX_X, ALU.add).then_inc(summed.sem, 1)
                dve.wait_ge(summed.sem, summed.count(it, n + 1))
                dve.scalar_tensor_tensor(cen[:, j, :, :], bc(mean[:, j, :], FEAT), -1.0 / FEAT, src, ALU.mult, ALU.add)\
                   .then_inc(centred.sem, 1)

            def variance(it, ln, j):
                dve.wait_ge(squared.sem, squared.count(it, ln * PAIRS + j + 1))
                dve.tensor_reduce(var[:, j, :], sq[:, j, :, :], AX_X, ALU.add).then_inc(var_ready.sem, 1)

            def attention(it, layer):
                def soften(k):
                    n = layer * GROUP + k
                    s = big[k % 2][0:HALF, 0:PAIR_TOKENS].rearrange("p (h t) -> p h t", h=2)
                    dve.wait_ge(scores_ready.sem, scores_ready.count(it, n + 1))
                    if layer == 1:
                        dve.tensor_tensor(prob[:, k % 4, :, :], s,
                                          P("bias").rearrange("p (h t) -> p h t", h=2), ALU.add).then_inc(biased.sem, 1)
                        dve.wait_ge(biased.sem, biased.count(it, k + 1))
                        s = prob[:, k % 4, :, :]
                    dve.tensor_reduce(peak[:, k % 4, :], s, AX_X, ALU.max).then_inc(peaked.sem, 1)
                    dve.wait_ge(peaked.sem, peaked.count(it, n + 1))
                    dve.tensor_tensor(prob[:, k % 4, :, :], s, bc(peak[:, k % 4, :], TOKENS), ALU.subtract)\
                       .then_inc(shifted.sem, 1)

                def divide(j):
                    n = layer * PAIRS + j
                    o = bank_o[0:HALF, 0:4 * AUG].rearrange("p (t e) -> p t e", t=4)
                    dst = (h1, att, u)[layer]
                    dve.wait_ge(out_ready.sem, out_ready.count(it, O_ATT[layer] * PAIRS + j + 1))
                    dve.reciprocal(rsum[:, j, :], o[:, :, FEAT]).then_inc(sum_inverted.sem, 1)
                    dve.wait_ge(sum_inverted.sem, sum_inverted.count(it, n + 1))
                    dve.tensor_tensor(dst[:, j, :, :], o[:, :, 0:FEAT], bc(rsum[:, j, :], FEAT), ALU.mult)\
                       .then_inc(bank_o_read.sem, 1)
                    done = bank_o_read.count(it, O_ATT[layer] * PAIRS + j + 1)
                    if layer < 2:
                        centre(it, (LN_IN, LN_ATT)[layer], j, dst[:, j, :, :], bank_o_read, done)
                    else:
                        dve.wait_ge(bank_o_read.sem, done)
                        dve.tensor_tensor(u[:, j, :, :], u[:, j, :, :], h3[:, j, :, :], ALU.add).then_inc(att_ready.sem, 1)
                        centre(it, LN_D, j, u[:, j, :, :], att_ready, att_ready.count(it, j + 1))

                first_ln = (LN_IN, LN_ATT, LN_D)[layer]
                for i in range(GROUP + 7):
                    if i % 2 == 0 and 0 <= (i - 6) // 2 < PAIRS:
                        divide((i - 6) // 2)
                    if 0 <= i - 2 < GROUP:
                        soften(i - 2)
                    if i % 2 == 0 and 0 <= (i - 6) // 2 < PAIRS:
                        variance(it, first_ln, (i - 6) // 2)
                if layer == 1:
                    for j in range(PAIRS):
                        centre(it, LN_B, j, u[:, j, :, :], gained, gained.count(it, 2 * j + 2))
                        variance(it, LN_B, j)

            def ffn(it):
                t = [0]

                def then_top(ins):
                    t[0] += 1
                    ins.then_inc(top_step.sem, 1)
                    dve.wait_ge(top_step.sem, top_step.count(it, t[0]))
                    hold(dve, dve_gate)

                dve.wait_ge(w_ready.sem, w_ready.count(it, 1))
                dve.tensor_copy(wcol[:, :, :], bank_g[0:HALF, 0:2 * GROUP].rearrange("p (h b) -> p h b", h=2))\
                   .then_inc(w_copied.sem, 1)
                dve.wait_ge(w_turned.sem, w_turned.count(it, 1))
                dve.tensor_copy(work[:, :], bank_v[0:GROUP, 0:TOKENS])
                then_top(dve.tensor_copy(wrow[:, :], bank_v[0:GROUP, 0:TOKENS]))
                for r in range(TOPK // 8):
                    then_top(dve.max(top8[:, :], work[:, :]))
                    then_top(dve.match_replace(work[:, :], top8[:, :], work[:, :], LOWEST))
                then_top(dve.max(top8[:, :], work[:, :]))
                then_top(dve.memset(top8[:, TOPK % 8:8], LOWEST))
                then_top(dve.match_replace(work[:, :], top8[:, :], work[:, :], LOWEST))
                then_top(dve.tensor_tensor(work[:, :], work[:, :], wrow[:, :], ALU.not_equal))
                then_top(dve.tensor_tensor(wmrow[:, :], work[:, :], wrow[:, :], ALU.mult))
                assert t[0] == 22
                dve.wait_ge(wm_turned.sem, wm_turned.count(it, 1))
                dve.tensor_copy(wm[:, :, :], bank_g[0:HALF, 64:64 + 2 * GROUP].rearrange("p (h b) -> p h b", h=2))\
                   .then_inc(wm_ready.sem, 1)
                for j in range(PAIRS):
                    dve.wait_ge(y_scaled.sem, y_scaled.count(it, 2 * j + 2))
                    dve.scalar_tensor_tensor(u[:, j, :, :], h2[:, j, :, :], 2.0, y[:, j, :, :], ALU.mult, ALU.add)\
                       .then_inc(u_ready.sem, 1)
                    centre(it, LN_FFN, j, u[:, j, :, :], u_ready, u_ready.count(it, j + 1))
                    variance(it, LN_FFN, j)

            def moe(it):
                def pick(j):
                    lg = bank_g[0:HALF, 0:4 * EXPERTS].rearrange("p (t e) -> p t e", t=4)
                    dve.wait_ge(logits_ready.sem, logits_ready.count(it, j + 1))
                    dve.tensor_reduce(lmax[:, j, 0, :], lg, AX_X, ALU.max).then_inc(route.sem, 1)
                    dve.wait_ge(route.sem, route.count(it, 4 * j + 1))
                    dve.tensor_tensor(hit[:, j, :, :], lg, bc(lmax[:, j, 0, :], EXPERTS), ALU.is_equal).then_inc(route.sem, 1)
                    dve.wait_ge(route.sem, route.count(it, 4 * j + 2))
                    dve.tensor_tensor(rank[:, j, :, :], hit[:, j, :, :], row(P("desc"), 4), ALU.mult).then_inc(route.sem, 1)
                    dve.wait_ge(route.sem, route.count(it, 4 * j + 3))
                    dve.tensor_reduce(lmax[:, j, 1, :], rank[:, j, :, :], AX_X, ALU.max).then_inc(route.sem, 1)
                    dve.wait_ge(route.sem, route.count(it, 4 * j + 4))
                    dve.tensor_tensor(cat[:, j, :, FEAT:CAT], rank[:, j, :, :], bc(lmax[:, j, 1, :], EXPERTS), ALU.is_equal)\
                       .then_inc(routed.sem, 1)

                def relu(j):
                    for c in (1, 3):
                        dve.wait_ge(ehid_ready.sem, ehid_ready.count(it, 4 * j + c + 1))
                        dve.tensor_scalar(ehid[:, j % 2, c, :], big[c][:, 0:PAIR_TOKENS], 0.0, None, ALU.max)\
                           .then_inc(relu_dve.sem, 1)

                def finish(j):
                    dve.wait_ge(out_ready.sem, out_ready.count(it, O_MOE * PAIRS + j + 1))
                    dve.scalar_tensor_tensor(u[:, j, :, :], bank_o[0:HALF, 0:4 * FEAT].rearrange("p (t e) -> p t e", t=4),
                                             0.0, cat[:, j, :, 0:FEAT], ALU.max, ALU.add).then_inc(bank_o_read.sem, 1)
                    centre(it, LN_MOE, j, u[:, j, :, :], bank_o_read, bank_o_read.count(it, O_MOE * PAIRS + j + 1))

                for i in range(PAIRS + 5):
                    if 0 <= i - 1 < PAIRS:
                        pick(i - 1)
                    if 0 <= i - 3 < PAIRS:
                        relu(i - 3)
                    if 0 <= i - 4 < PAIRS:
                        finish(i - 4)
                        variance(it, LN_MOE, i - 4)

            with dve.Fori(0, ITERS) as it:
                attention(it, 0)
                attention(it, 1)
                ffn(it)
                attention(it, 2)
                moe(it)

        @block.gpsimd
        def _(pool):
            for last in stored:
                pool.sem_inc(last.sem, last.head)
            pool.wait_ge(setup_done.sem, 1)

            def square(it, ln, j):
                pool.wait_ge(centred.sem, centred.count(it, ln * PAIRS + j + 1))
                pool.tensor_tensor(sq[:, j, :, :], cen[:, j, :, :], cen[:, j, :, :], ALU.mult).then_inc(squared.sem, 1)

            def scale(it, ln, j, dst):
                n = ln * PAIRS + j
                pool.wait_ge(var_ready.sem, var_ready.count(it, n + 1))
                hold(pool, pool_gate)
                pool.tensor_scalar(rstd[:, j, :], var[:, j, :], 1.0 / FEAT, EPS, ALU.mult, ALU.add).then_inc(var_eps.sem, 1)
                pool.wait_ge(var_eps.sem, var_eps.count(it, n + 1))
                pool.tensor_tensor(rstd[:, j, :], rstd[:, j, :], neg_half[:, :], ALU.pow).then_inc(rstd_ready.sem, 1)
                pool.wait_ge(rstd_ready.sem, rstd_ready.count(it, n + 1))
                pool.tensor_tensor(dst, cen[:, j, :, :], bc(rstd[:, j, :], FEAT), ALU.mult).then_inc(normed.sem, 1)

            with pool.Fori(0, ITERS) as it:
                for j in range(PAIRS):
                    square(it, LN_IN, j)
                    scale(it, LN_IN, j, xn[:, j, :, :])
                for j in range(PAIRS):
                    pool.tensor_tensor(resid[:, j, :, :], h1[:, j, :, :], row(P("b2"), 4), ALU.add).then_inc(res_ready.sem, 1)
                for j in range(PAIRS):
                    square(it, LN_ATT, j)
                    scale(it, LN_ATT, j, on[:, j, :, :])
                    pool.wait_ge(normed.sem, normed.count(it, LN_ATT * PAIRS + j + 1))
                    pool.tensor_tensor(on[:, j, :, :], on[:, j, :, :], row(P("g2"), 4), ALU.mult).then_inc(gained.sem, 1)
                    pool.wait_ge(gained.sem, gained.count(it, 2 * j + 1))
                    pool.wait_ge(res_ready.sem, res_ready.count(it, j + 1))
                    pool.tensor_tensor(u[:, j, :, :], on[:, j, :, :], resid[:, j, :, :], ALU.add).then_inc(gained.sem, 1)
                for j in range(PAIRS):
                    square(it, LN_B, j)
                    scale(it, LN_B, j, h2[:, j, :, :])
                for j in range(PAIRS):
                    pool.wait_ge(bank_o_read.sem, bank_o_read.count(it, O_FFN * PAIRS + j + 1))
                    pool.tensor_tensor(y[:, j, :, :], y[:, j, :, :], row(P("fb2"), 4), ALU.add).then_inc(y_scaled.sem, 1)
                    if j == 0:
                        pool.wait_ge(wm_ready.sem, wm_ready.count(it, 1))
                    pool.wait_ge(y_scaled.sem, y_scaled.count(it, 2 * j + 1))
                    w = wm[:, :, 2 * j:2 * j + 2].rearrange("p h b -> p b h").unsqueeze(3).to_broadcast([HALF, 2, 2, FEAT])
                    y4 = y[:, j, :, :].rearrange("p (b h) e -> p b h e", b=2)
                    pool.tensor_tensor(y4, y4, w, ALU.mult).then_inc(y_scaled.sem, 1)
                for j in range(PAIRS):
                    square(it, LN_FFN, j)
                    scale(it, LN_FFN, j, h3[:, j, :, :])
                for j in range(PAIRS):
                    square(it, LN_D, j)
                    scale(it, LN_D, j, cat[:, j, :, 0:FEAT])
                for j in range(PAIRS):
                    square(it, LN_MOE, j)
                    pool.wait_ge(stored[j].sem, stored[j].count(it, 0))
                    scale(it, LN_MOE, j, res[:, j, :, :])


def _lay_out(inputs):
    f = {k: np.ascontiguousarray(np.asarray(v), dtype=np.float32) for k, v in inputs.items()}
    x = f["x"].reshape(IMAGES, 48, 2, 48, 2).transpose(2, 4, 0, 1, 3)
    x = x.reshape(2, 2, IMAGES, PER_CHANNEL, FEAT).transpose(1, 4, 0, 2, 3)
    pixels = np.ascontiguousarray(x).reshape(2 * FEAT, 2, IMAGES, PER_CHANNEL)

    par = np.zeros((128, PARAM_COLS), np.float32)

    def put(name, array, row=0, col=0):
        a = np.asarray(array, np.float32)
        c = START[name] + col
        par[row:row + a.shape[0], c:c + a.shape[1]] = a

    def rep(vector, rows):
        return np.broadcast_to(vector.reshape(1, -1), (rows, vector.size))

    put("ident", np.eye(128))
    put("eye2", np.eye(FEAT))
    put("eye2", np.eye(FEAT), row=FEAT)
    cw = f["L0_tok_conv_w"].reshape(CHANNELS, 2, 2)
    for b in range(2):
        put("convw", rep(cw[:, :, b], FEAT), row=b * FEAT)
    put("convb", rep(f["L0_tok_conv_b"], FEAT))
    pos = np.arange(TOKENS, dtype=np.float64)
    put("xinit", np.ones((1, TOKENS)), row=ONE)
    for n, period in enumerate(SCALES):
        put("xinit", np.stack([np.cos(2 * np.pi * pos / period), np.sin(2 * np.pi * pos / period)]), row=AUG + 2 * n)
    for name, w, b in (("wqA", "L0_tok_wq", "L0_tok_bq"), ("wkA", "L0_tok_wk", "L0_tok_bk"), ("wvA", "L0_tok_wv", "L0_tok_bv"),
                       ("wqD", "L1_attn_Wq", "L1_attn_bq"), ("wkD", "L1_attn_Wk", "L1_attn_bk")):
        put(name, f[w])
        put(name, f[b][:, None], col=FEAT)
    put("woA", f["L0_tok_wo"].T)
    put("vaddA", f["L0_tok_bo"][None], row=ONE)
    put("vaddA", np.ones((1, 1)), row=ONE, col=FEAT)
    qkv = f["L0_attn_qkv_w"].T
    for n, name in enumerate(("wqB", "wkB", "wvB")):
        put(name, qkv[n * FEAT:(n + 1) * FEAT])
        put("qkvb", f["L0_attn_qkv_b"][n * FEAT:(n + 1) * FEAT, None], col=n)
    put("g1", rep(f["L0_attn_ln1_g"], FEAT))
    put("b1", rep(f["L0_attn_ln1_b"], FEAT))
    put("projB", f["L0_attn_proj_w"])
    put("scaleB", rep(f["L0_attn_scale"].reshape(1), 128))
    put("vaddB", f["L0_attn_proj_b"][None], row=ONE)
    put("vaddB", np.ones((1, 1)), row=ONE, col=FEAT)
    put("g2", rep(f["L0_attn_ln2_g"], HALF))
    put("b2", rep(f["L0_attn_ln2_b"], HALF))
    table = f["L0_attn_bias_table"]
    key = np.arange(TOKENS)
    for h in range(2):
        query = h * HALF + np.arange(HALF)
        put("bias", table[key[None, :] - query[:, None] + TOKENS - 1], col=h * TOKENS)
    put("wr", f["L0_ffn_wr"])
    put("wr", f["L0_ffn_br"][None], row=ONE)
    put("w1", f["L0_ffn_w1"])
    put("w1", f["L0_ffn_b1"][None], row=ONE)
    for c in range(2):
        put("w2", f["L0_ffn_w2"][c * 128:(c + 1) * 128], col=c * FEAT)
    put("fb2", rep(f["L0_ffn_b2"], HALF))
    for n in range(2):
        for r in range(2):
            put("betaD", f["L1_attn_beta"][n].reshape(1, 1), row=AUG + 2 * n + r, col=AUG + 2 * n + r)
    put("vD", f["L1_attn_Wv"].T)
    put("vD", f["L1_attn_bv"][None], row=ONE)
    put("vD", np.ones((1, 1)), row=ONE, col=FEAT)
    put("router", f["L1_ffn_router_w"].T)
    put("router", f["L1_ffn_router_b"][None], row=ONE)
    put("ew1", f["L1_ffn_W1"].transpose(1, 0, 2).reshape(FEAT, MOE_H))
    put("ew1", np.full((EXPERTS, MOE_H), OFF), row=FEAT)
    for e in range(EXPERTS):
        put("ew1", f["L1_ffn_b1"][e][None], row=FEAT + e, col=e * HIDDEN)
    w2 = f["L1_ffn_W2"].reshape(MOE_H, FEAT)
    for c in range(4):
        put("ew2", w2[c * 128:(c + 1) * 128], col=c * FEAT)
    put("eb2", f["L1_ffn_b2"], row=FEAT)
    put("desc", rep(np.arange(EXPERTS, 0, -1), HALF))
    return pixels, par


def kernel(**inputs):
    import concourse.bacc as bacc
    from concourse.bass_utils import run_bass_kernel_spmd

    pixels, par = _lay_out(inputs)
    nc = bacc.Bacc("TRN2", target_bir_lowering=False, num_devices=1)
    pixels_dram = nc.dram_tensor("pixels", pixels.shape, F32, kind="ExternalInput").ap()
    params_dram = nc.dram_tensor("params", par.shape, F32, kind="ExternalInput").ap()
    out_dram = nc.dram_tensor("out", (IMAGES, TOKENS, FEAT), F32, kind="ExternalOutput").ap()
    build(nc, pixels_dram, params_dram, out_dram)
    r = run_bass_kernel_spmd(nc, [{"pixels": pixels, "params": par}], core_ids=[0])
    return r.results[0]["out"]
```

```python
from contextlib import ExitStack

import concourse.bass as bass
from concourse import mybir
import numpy as np

F32 = mybir.dt.float32
ALU = mybir.AluOpType
ACT = mybir.ActivationFunctionType
AX_X = mybir.AxisListType.X

IMAGES, TOKENS, FEAT = 64, 144, 64
HALF = TOKENS // 2
GROUP = 8
ITERS = IMAGES // GROUP
PAIRS = GROUP // 2
PAIR_TOKENS = 2 * TOKENS
CHANNELS = 4
PER_CHANNEL = TOKENS // CHANNELS
ONE = FEAT
AUG = FEAT + 1
SCALES = (24.0, 720.0)
AUGC = AUG + 2 * len(SCALES)
ROWS = 128
EXPERTS, HIDDEN = 32, 16
MOE_H = EXPERTS * HIDDEN
CAT = FEAT + EXPERTS
FFN_H = 4 * FEAT
TOPK = TOKENS // 2 - 1
OFF = -1.0e30
LOWEST = -3.4028234663852886e38
EPS = 1e-5

SECTIONS = dict(
    ident=(128, 128), eye2=(128, FEAT), convw=(128, 2 * CHANNELS), convb=(FEAT, CHANNELS), xinit=(ROWS, TOKENS),
    wqA=(FEAT, ROWS), wkA=(FEAT, ROWS), wvA=(FEAT, ROWS), woA=(FEAT, FEAT), vaddA=(ROWS, AUG),
    wqB=(FEAT, FEAT), wkB=(FEAT, FEAT), wvB=(FEAT, FEAT), qkvb=(FEAT, 3), g1=(FEAT, FEAT), b1=(FEAT, FEAT),
    projB=(FEAT, FEAT), scaleB=(128, 1), vaddB=(ROWS, AUG), g2=(HALF, FEAT), b2=(HALF, FEAT),
    bias=(HALF, PAIR_TOKENS),
    wr=(ROWS, 1), w1=(ROWS, FFN_H), w2=(128, 2 * FEAT), fb2=(HALF, FEAT),
    wqD=(FEAT, ROWS), wkD=(FEAT, ROWS), betaD=(ROWS, ROWS), vD=(ROWS, AUG),
    router=(ROWS, EXPERTS), ew1=(ROWS, MOE_H), ew2=(128, 4 * FEAT), eb2=(CAT, FEAT), desc=(HALF, EXPERTS),
)
START = {}
_at = 0
for _name, (_rows, _cols) in SECTIONS.items():
    START[_name] = _at
    _at += _cols
PARAM_COLS = _at


class When:

    def __init__(self, reg, ahead=0):
        self.reg, self.ahead = reg, ahead


class Step:

    def __init__(self, sem, per, head):
        self.sem, self.per, self.head = sem, per, head

    def count(self, when, n):
        return when.reg * self.per + (when.ahead * self.per + n + self.head)


def build(nc, pixels, params, out):
    with ExitStack() as ctx:
        def sb(name, shape):
            return ctx.enter_context(nc.sbuf_tensor(name, shape, F32))

        def step(name, per, head=0):
            return Step(ctx.enter_context(nc.semaphore(name)), per, head)

        par = sb("par", [128, PARAM_COLS])

        def P(name, c0=0, c1=None):
            rows, cols = SECTIONS[name]
            return par[0:rows, START[name] + c0:START[name] + (cols if c1 is None else c1)]

        class Stream:

            def __init__(self, tag, layers, norms):
                self.xT = sb("xT" + tag, [ROWS, GROUP, TOKENS])
                self.gT = sb("gT" + tag, [ROWS, 2, PAIR_TOKENS])
                self.val = sb("val" + tag, [ROWS, 4, 4, AUG])
                self.prob = sb("prob" + tag, [HALF, 4, 2, TOKENS])
                self.probT = sb("probT" + tag, [ROWS, 2, 2, TOKENS])
                self.peak = sb("peak" + tag, [HALF, 4, 2])
                self.rsum = sb("rsum" + tag, [HALF, 4, 4])
                self.u = sb("u" + tag, [HALF, 4, 4, FEAT])
                self.cen = sb("cen" + tag, [HALF, 4, 4, FEAT])
                self.sq = sb("sq" + tag, [HALF, 4, 4, FEAT])
                self.mean = sb("mean" + tag, [HALF, 4, 4])
                self.var = sb("var" + tag, [HALF, 4, 4])
                self.rstd = sb("rstd" + tag, [HALF, 4, 4])
                banks = ctx.enter_context(nc.psum_tensor("banks" + tag, [128, 4, 512], F32))
                self.bank = [banks[:, b, 0:PAIR_TOKENS] for b in range(4)]
                self.bank_s, self.bank_p, self.bank_g, self.bank_o = self.bank

                def outputs(width):
                    return banks[0:HALF, 3, 0:4 * width].rearrange("p (b h e) -> p b h e", b=2, h=2)

                self.outputs = outputs
                turns, outs = (2, 2) if tag == "a" else (2, 3)
                self.turned = step("turned_" + tag, turns * PAIRS)
                self.x_ready = step("x_ready_" + tag, turns * PAIRS)
                self.g_ready = step("g_ready_" + tag, layers * PAIRS)
                self.g_copied = step("g_copied_" + tag, layers * PAIRS)
                self.v_ready = step("v_ready_" + tag, layers * PAIRS)
                self.v_copied = step("v_copied_" + tag, layers * PAIRS)
                self.scores_ready = step("scores_ready_" + tag, layers * GROUP)
                self.peaked = step("peaked_" + tag, layers * GROUP)
                self.shifted = step("shifted_" + tag, layers * GROUP)
                self.exp_done = step("exp_done_" + tag, layers * GROUP)
                self.probs_turned = step("probs_turned_" + tag, layers * GROUP)
                self.probT_ready = step("probT_ready_" + tag, layers * GROUP)
                self.out_ready = step("out_ready_" + tag, outs * PAIRS)
                self.out_read = step("out_read_" + tag, outs * PAIRS, 1)
                self.sum_inverted = step("sum_inverted_" + tag, layers * PAIRS)
                self.summed = [step(f"summed_{tag}{n}", PAIRS) for n in range(norms)]
                self.centred = [step(f"centred_{tag}{n}", PAIRS) for n in range(norms)]
                self.squared = [step(f"squared_{tag}{n}", PAIRS) for n in range(norms)]
                self.var_ready = [step(f"var_ready_{tag}{n}", PAIRS) for n in range(norms)]
                self.var_eps = [step(f"var_eps_{tag}{n}", PAIRS) for n in range(norms)]
                self.rstd_ready = [step(f"rstd_ready_{tag}{n}", PAIRS) for n in range(norms)]
                self.normed = [step(f"normed_{tag}{n}", PAIRS) for n in range(norms)]

        LN_IN, LN_ATT, LN_B = range(3)
        LN_FFN, LN_D, LN_MOE = range(3)
        T_IN, T_FFN = range(2)
        T_ATT, T_MOE = range(2)
        O_FFN, O_ATT, O_MOE = range(3)
        A, B = Stream("a", 2, 3), Stream("b", 1, 3)

        conv_lhs = sb("conv_lhs", [128, CHANNELS, 2, FEAT])
        a_mat = [sb(f"a_mat{n}", [ROWS, ROWS]) for n in range(3)]
        v_mat = [sb(f"v_mat{n}", [ROWS, AUG]) for n in range(2)]
        qkv_fold = sb("qkv_fold", [FEAT, 3, ROWS])
        qkv_sum = sb("qkv_sum", [FEAT, 3])
        fold_tmp = sb("fold_tmp", [FEAT, 3, FEAT])
        neg_half = sb("neg_half", [HALF, 4])

        pix = sb("pix", [128, 2, GROUP, PER_CHANNEL])
        featT = sb("featT", [ROWS, GROUP, TOKENS])
        h2T = sb("h2T", [ROWS, GROUP, TOKENS])
        att = sb("att", [HALF, 4, 4, FEAT])
        h1 = sb("h1", [HALF, 4, 4, FEAT])
        h2 = sb("h2", [HALF, 4, 4, FEAT])
        h3 = sb("h3", [HALF, 4, 4, FEAT])
        xn = sb("xn", [HALF, 4, 4, FEAT])
        on = sb("on", [HALF, 4, 4, FEAT])
        y = sb("y", [HALF, 4, 4, FEAT])
        resid = sb("resid", [HALF, 4, 4, FEAT])
        res = sb("res", [HALF, 4, 4, FEAT])
        cat = sb("cat", [HALF, 4, 4, CAT])
        hid = sb("hid", [128, 2, 2, PAIR_TOKENS])
        wcol = sb("wcol", [HALF, 2, GROUP])
        wrow = sb("wrow", [GROUP, TOKENS])
        work = sb("work", [GROUP, TOKENS])
        top8 = sb("top8", [GROUP, 8])
        wmrow = sb("wmrow", [GROUP, TOKENS])
        wm = sb("wm", [HALF, 2, GROUP])
        lmax = sb("lmax", [HALF, 4, 2, 4])
        hit = sb("hit", [HALF, 4, 4, EXPERTS])
        rank = sb("rank", [HALF, 4, 4, EXPERTS])
        catT = sb("catT", [ROWS, 3, PAIR_TOKENS])
        ehid = sb("ehid", [128, 2, 4, PAIR_TOKENS])

        params_in = step("params_in", 0)
        folded_dve = step("folded_dve", 0)
        padded = step("padded", 0)
        folded_pe = step("folded_pe", 0)
        setup_done = step("setup_done", 0)
        pixels_in = step("pixels_in", 16)
        conv_ready = step("conv_ready", CHANNELS)
        feat_ready = step("feat_ready", CHANNELS)
        biased = step("biased", GROUP)
        att_ready = step("att_ready", PAIRS)
        u_ready = step("u_ready", PAIRS)
        gained = step("gained", 2 * PAIRS)
        res_ready = step("res_ready", PAIRS)
        w_ready = step("w_ready", 1)
        w_copied = step("w_copied", 1, head=1)
        w_turned = step("w_turned", 1)
        TOP_STEPS = 2 * (TOPK // 8) + 6
        top_step = step("top_step", TOP_STEPS)
        wm_turned = step("wm_turned", 1)
        wm_ready = step("wm_ready", 1)
        hid_ready = step("hid_ready", 2 * PAIRS)
        gelu_done = step("gelu_done", 2 * PAIRS)
        y_biased = step("y_biased", PAIRS)
        y_scaled = step("y_scaled", PAIRS)
        logits_ready = step("logits_ready", PAIRS)
        route = step("route", 4 * PAIRS)
        routed = step("routed", PAIRS)
        cat_turned = step("cat_turned", PAIRS)
        catT_ready = step("catT_ready", PAIRS)
        ehid_ready = step("ehid_ready", 4 * PAIRS)
        relu_act = step("relu_act", 2 * PAIRS)
        relu_dve = step("relu_dve", 2 * PAIRS)
        stored = [step(f"stored{j}", 16, head=16) for j in range(PAIRS)]
        pe_gate = step("pe_gate", 0)
        dve_gate = step("dve_gate", 0)
        pool_gate = step("pool_gate", 0)

        def hold(eng, gate):
            eng.sem_inc(gate.sem, 1)

        block = ctx.enter_context(nc.Block())

        def bc(ap2, n):
            return ap2.unsqueeze(2).to_broadcast([ap2.shape[0], ap2.shape[1], n])

        def row(ap2, n):
            return ap2.unsqueeze(1).to_broadcast([ap2.shape[0], n, ap2.shape[1]])

        def pairwise(ap3):
            return ap3.rearrange("p (b h) e -> p b h e", b=2)

        AT_CONV, AT_ATT0, AT_ATT1, AT_ROUTER = 0, 1, 10, 22
        AT_FFN, AT_ATT2, AT_MOE = 0, 6, 15
        SLOTS = 30

        def pair_at(i, first, every=2):
            j, rest = divmod(i - first, every)
            return j if rest == 0 and 0 <= j < PAIRS else None

        PHASES = 4

        def run(eng, half_a, half_b):
            for i in range(SLOTS):
                for phase in range(PHASES):
                    half_a(When(0), i, phase)
            with eng.Fori(0, ITERS - 1) as g:
                for i in range(SLOTS):
                    for phase in range(PHASES):
                        half_b(When(g), i, phase)
                        half_a(When(g, 1), i, phase)
            for i in range(SLOTS):
                for phase in range(PHASES):
                    half_b(When(0, ITERS - 1), i, phase)

        @block.sync
        def _(sp):
            sp.dma_start(par[:, :], params[:, :]).then_inc(params_in.sem, 16)
            sp.dma_start(pix[:, :, :, :], pixels[:, :, 0:GROUP, :]).then_inc(pixels_in.sem, 16)

            def load_after(when, group):
                sp.wait_ge(conv_ready.sem, conv_ready.count(when, CHANNELS))
                sp.dma_start(pix[:, :, :, :], pixels[:, :, group, :]).then_inc(pixels_in.sem, 16)

            def store(when, group):
                for j in range(PAIRS):
                    sp.wait_ge(B.normed[LN_MOE].sem, B.normed[LN_MOE].count(when, j + 1))
                    dst = out[bass.ds(group * GROUP + 2 * j, 2), :, :].rearrange("b (h p) d -> p (b h) d", p=HALF)
                    sp.dma_start(dst, res[:, j, :, :]).then_inc(stored[j].sem, 16)

            load_after(When(0), slice(GROUP, 2 * GROUP))
            with sp.Fori(0, ITERS - 2) as g:
                load_after(When(g, 1), bass.ds((g + 2) * GROUP, GROUP))
                store(When(g), g)
            store(When(0, ITERS - 2), ITERS - 2)
            store(When(0, ITERS - 1), ITERS - 1)
            for j in range(PAIRS):
                sp.wait_ge(stored[j].sem, 16 * (ITERS + 1))

        @block.tensor
        def _(pe):
            for head_start in (A.out_read, B.out_read, w_copied):
                pe.sem_inc(head_start.sem, head_start.head)
            pe.wait_ge(params_in.sem, 16)
            pe.matmul(A.bank[0][:, 0:ROWS], P("wqA"), P("wkA"), start=True, stop=True)
            pe.matmul(A.bank[1][:, 0:ROWS], P("wqD"), P("wkD"), start=True, stop=True)
            pe.matmul(A.bank[2][:, 0:FEAT], P("wvA"), P("woA"), start=True, stop=True).then_inc(folded_pe.sem, 1)
            pe.wait_ge(folded_dve.sem, 3)
            pe.matmul(B.bank[0][:, 0:ROWS], qkv_fold[:, 0, :], qkv_fold[:, 1, :], start=True, stop=True)
            pe.matmul(B.bank[1][:, 0:FEAT], qkv_fold[:, 2, :], P("projB"), start=True, stop=True)\
              .then_inc(folded_pe.sem, 1)
            pe.wait_ge(setup_done.sem, 1)
            pe.wait_ge(padded.sem, 1)

            def conv(it):
                pe.wait_ge(pixels_in.sem, pixels_in.count(it, 16))
                pe.wait_ge(w_copied.sem, w_copied.count(it, 0))
                for c in range(CHANNELS):
                    for a in range(2):
                        mm = pe.matmul(A.bank[c][0:FEAT, :], conv_lhs[:, c, a, :], pix[:, a, :, :],
                                       start=a == 0, stop=a == 1)
                    mm.then_inc(conv_ready.sem, 1)

            def turn(it, st, src, ln_of, ln, j, bank_free):
                pe.wait_ge(ln_of.normed[ln].sem, ln_of.normed[ln].count(it, j + 1))
                if bank_free is not None:
                    pe.wait_ge(bank_free[0].sem, bank_free[0].count(it, bank_free[1]))
                hold(pe, pe_gate)
                for t in range(4):
                    mm = pe.transpose(st.bank_g[0:FEAT, t * HALF:(t + 1) * HALF], src[:, t, :], P("ident")[0:HALF, 0:HALF])
                mm.then_inc(st.turned.sem, 1)

            def attention(it, st, layer, out_at, src, am, vw, src_ready, turn_pair, i, phase):

                def project_g(j):
                    n = layer * PAIRS + j
                    sem, need = src_ready(j)
                    pe.wait_ge(sem, need)
                    if turn_pair is None and j >= 1:
                        pe.wait_ge(st.v_copied.sem, st.v_copied.count(it, n))
                    pe.matmul(st.bank_g[:, :], am[:, :], src[:, 2 * j:2 * j + 2, :],
                              start=True, stop=True).then_inc(st.g_ready.sem, 1)

                def project_v(j):
                    n = layer * PAIRS + j
                    pe.wait_ge(st.g_copied.sem, st.g_copied.count(it, n + 1))
                    for t in range(4):
                        mm = pe.matmul(st.bank_g[0:HALF, t * AUG:(t + 1) * AUG],
                                       src[:, 2 * j + t // 2, (t % 2) * HALF:(t % 2 + 1) * HALF], vw,
                                       start=True, stop=True)
                    mm.then_inc(st.v_ready.sem, 1)

                def scores(k):
                    n = layer * GROUP + k
                    pe.wait_ge(st.g_copied.sem, st.g_copied.count(it, layer * PAIRS + k // 2 + 1))
                    if am is a_mat[1] and k >= 1:
                        pe.wait_ge(biased.sem, biased.count(it, k))
                    elif n >= 1:
                        pe.wait_ge(st.shifted.sem, st.shifted.count(it, n))
                    for h in range(2):
                        c = (k % 2) * TOKENS + h * HALF
                        mm = pe.matmul(st.bank_s[0:HALF, h * TOKENS:(h + 1) * TOKENS],
                                       st.gT[:, (k // 2) % 2, c:c + HALF], src[:, k, :], start=True, stop=True)
                    mm.then_inc(st.scores_ready.sem, 1)

                def turn_probs(k):
                    n = layer * GROUP + k
                    pe.wait_ge(st.exp_done.sem, st.exp_done.count(it, n + 1))
                    if n >= 1:
                        pe.wait_ge(st.probT_ready.sem, st.probT_ready.count(it, n))
                    for th in range(2):
                        for sh in range(2):
                            c = th * TOKENS + sh * HALF
                            mm = pe.transpose(st.bank_p[0:HALF, c:c + HALF],
                                              st.prob[:, k % 4, sh, th * HALF:(th + 1) * HALF], P("ident")[0:HALF, 0:HALF])
                    mm.then_inc(st.probs_turned.sem, 1)

                def weigh(k):
                    j = k // 2
                    pe.wait_ge(st.probT_ready.sem, st.probT_ready.count(it, layer * GROUP + k + 1))
                    pe.wait_ge(st.v_copied.sem, st.v_copied.count(it, layer * PAIRS + j + 1))
                    if k % 2 == 0:
                        pe.wait_ge(st.out_read.sem, st.out_read.count(it, out_at * PAIRS + j))
                    for sh in range(2):
                        for th in range(2):
                            mm = pe.matmul(st.outputs(AUG)[:, k % 2, sh, :],
                                           st.probT[:, k % 2, th, sh * HALF:(sh + 1) * HALF],
                                           st.val[:, j, (k % 2) * 2 + th, :], start=th == 0, stop=th == 1)
                    if k % 2 == 1:
                        mm.then_inc(st.out_ready.sem, 1)

                if phase == 0 and pair_at(i, 2) is not None:
                    project_v(pair_at(i, 2))
                if phase == 0 and 0 <= i - 2 < GROUP:
                    scores(i - 2)
                if phase == 1 and pair_at(i, 1) is not None:
                    project_g(pair_at(i, 1))
                if phase == 2 and 0 <= i - 5 < GROUP:
                    weigh(i - 5)
                if phase == 3 and 0 <= i - 4 < GROUP:
                    turn_probs(i - 4)
                if phase == 3 and turn_pair is not None and pair_at(i, 0) is not None:
                    turn_pair(pair_at(i, 0))

            def router(it, i, phase):
                j = pair_at(i, 1)
                if phase == 3 and j is not None:
                    pe.wait_ge(A.x_ready.sem, A.x_ready.count(it, T_FFN * PAIRS + j + 1))
                    if j == 0:
                        pe.wait_ge(A.out_read.sem, A.out_read.count(it, 2 * PAIRS))
                    for t in range(4):
                        col = (t % 2) * GROUP + 2 * j + t // 2
                        mm = pe.matmul(A.bank_o[0:HALF, col:col + 1],
                                       h2T[:, 2 * j + t // 2, (t % 2) * HALF:(t % 2 + 1) * HALF], P("wr"),
                                       start=True, stop=True)
                    if j == PAIRS - 1:
                        mm.then_inc(w_ready.sem, 1)
                j = pair_at(i, 0)
                if phase == 3 and j is not None:
                    turn(it, A, h2[:, j, :, :], A, LN_B, j, (A.x_ready, T_FFN * PAIRS + j) if j else (A.v_copied, 2 * PAIRS))

            def ffn(it, i, phase):
                def hidden(j):
                    for c in range(2):
                        n = 2 * j + c
                        if n >= 2:
                            pe.wait_ge(gelu_done.sem, gelu_done.count(it, n - 1))
                        pe.matmul(B.bank[c][:, :], P("w1", 128 * c, 128 * (c + 1)),
                                  h2T[:, 2 * j:2 * j + 2, :], start=True, stop=True).then_inc(hid_ready.sem, 1)

                def second(j):
                    pe.wait_ge(gelu_done.sem, gelu_done.count(it, 2 * j + 2))
                    pe.wait_ge(B.out_read.sem, B.out_read.count(it, O_FFN * PAIRS + j))
                    for t in range(4):
                        for c in range(2):
                            mm = pe.matmul(B.outputs(FEAT)[:, t // 2, t % 2, :],
                                           hid[:, j % 2, c, t * HALF:(t + 1) * HALF], P("w2", c * FEAT, (c + 1) * FEAT),
                                           start=c == 0, stop=c == 1)
                    mm.then_inc(B.out_ready.sem, 1)

                if phase == 0 and i == 0:
                    pe.wait_ge(w_copied.sem, w_copied.count(it, 1))
                    for h in range(2):
                        mm = pe.transpose(B.bank_g[0:GROUP, 32 + h * HALF:32 + (h + 1) * HALF], wcol[:, h, :],
                                          P("ident")[0:HALF, 0:HALF])
                    mm.then_inc(w_turned.sem, 1)
                if phase == 0 and pair_at(i, 0, 1) is not None:
                    hidden(i)
                if phase == 2 and pair_at(i, 1, 1) is not None:
                    second(i - 1)
                if phase == 0 and i == 3:
                    pe.wait_ge(top_step.sem, top_step.count(it, TOP_STEPS))
                    hold(pe, pe_gate)
                    for h in range(2):
                        mm = pe.transpose(B.bank_g[0:HALF, 192 + h * GROUP:192 + (h + 1) * GROUP],
                                          wmrow[:, h * HALF:(h + 1) * HALF], P("ident")[0:GROUP, 0:GROUP])
                    mm.then_inc(wm_turned.sem, 1)

            def moe(it, i, phase):
                def logits(j):
                    pe.wait_ge(B.x_ready.sem, B.x_ready.count(it, T_MOE * PAIRS + j + 1))
                    for t in range(4):
                        mm = pe.matmul(B.bank_g[0:HALF, t * EXPERTS:(t + 1) * EXPERTS],
                                       B.xT[:, 2 * j + t // 2, (t % 2) * HALF:(t % 2 + 1) * HALF], P("router"),
                                       start=True, stop=True)
                    mm.then_inc(logits_ready.sem, 1)

                def turn_cat(j):
                    pe.wait_ge(routed.sem, routed.count(it, j + 1))
                    for t in range(4):
                        mm = pe.transpose(B.bank_g[0:CAT, t * HALF:(t + 1) * HALF], cat[:, j, t, :],
                                          P("ident")[0:HALF, 0:HALF])
                    mm.then_inc(cat_turned.sem, 1)

                def hidden(j, c):
                    if c == 0:
                        pe.wait_ge(catT_ready.sem, catT_ready.count(it, j + 1))
                    n = 2 * j + c // 2
                    if n >= 1:
                        done = relu_dve if c % 2 else relu_act
                        pe.wait_ge(done.sem, done.count(it, n))
                    pe.matmul(B.bank[c % 2][:, :], P("ew1", 128 * c, 128 * (c + 1)),
                              catT[:, j % 3, :], start=True, stop=True).then_inc(ehid_ready.sem, 1)

                def second(j):
                    pe.wait_ge(relu_act.sem, relu_act.count(it, 2 * j + 2))
                    pe.wait_ge(relu_dve.sem, relu_dve.count(it, 2 * j + 2))
                    pe.wait_ge(B.out_read.sem, B.out_read.count(it, O_MOE * PAIRS + j))
                    for t in range(4):
                        for c in range(4):
                            pe.matmul(B.outputs(FEAT)[:, t // 2, t % 2, :],
                                      ehid[:, j % 2, c, t * HALF:(t + 1) * HALF], P("ew2", c * FEAT, (c + 1) * FEAT),
                                      start=c == 0, stop=False)
                        mm = pe.matmul(B.outputs(FEAT)[:, t // 2, t % 2, :],
                                       catT[FEAT:CAT, j % 3, t * HALF:(t + 1) * HALF], P("eb2")[FEAT:CAT, :],
                                       start=False, stop=True)
                    mm.then_inc(B.out_ready.sem, 1)

                j = pair_at(i, 1)
                if phase == 0 and j is not None:
                    logits(j)
                j = pair_at(i, 2)
                if phase == 0 and j is not None:
                    turn_cat(j)
                j = pair_at(i, 3)
                if phase == 1 and j is not None:
                    hidden(j, 0)
                    hidden(j, 1)
                j = pair_at(i, 4)
                if phase == 1 and j is not None:
                    hidden(j, 2)
                    hidden(j, 3)
                j = pair_at(i, 5)
                if phase == 2 and j is not None:
                    second(j)
                j = pair_at(i, 0)
                if phase == 3 and j is not None:
                    turn(it, B, cat[:, j, :, 0:FEAT], B, LN_D, j, (catT_ready, j) if j else (B.v_copied, PAIRS))

            def half_a(it, i, phase):
                if phase == 0 and i == AT_CONV:
                    conv(it)
                attention(it, A, 0, 0, featT, a_mat[0], v_mat[0][:, :],
                          lambda j: (feat_ready.sem, feat_ready.count(it, CHANNELS)), None, i - AT_ATT0, phase)
                attention(it, A, 1, 1, A.xT, a_mat[1], v_mat[1][:, :],
                          lambda j: (A.x_ready.sem, A.x_ready.count(it, j + 1)),
                          lambda j: turn(it, A, xn[:, j, :, :], A, LN_IN, j, (A.v_copied, PAIRS + j)), i - AT_ATT1, phase)
                router(it, i - AT_ROUTER, phase)

            def half_b(it, i, phase):
                ffn(it, i - AT_FFN, phase)
                attention(it, B, 0, O_ATT, B.xT, a_mat[2], P("vD"),
                          lambda j: (B.x_ready.sem, B.x_ready.count(it, T_ATT * PAIRS + j + 1)),
                          lambda j: turn(it, B, h3[:, j, :, :], B, LN_FFN, j, (B.v_copied, j) if j else None), i - AT_ATT2, phase)
                moe(it, i - AT_MOE, phase)

            run(pe, half_a, half_b)

        @block.scalar
        def _(act):
            def copy_x(it, st, stage, j, dst):
                act.wait_ge(st.turned.sem, st.turned.count(it, stage * PAIRS + j + 1))
                act.copy(dst[0:FEAT, 2 * j:2 * j + 2, :], st.bank_g[0:FEAT, :].rearrange("p (b s) -> p b s", b=2))\
                   .then_inc(st.x_ready.sem, 1)

            def square(it, st, ln, j):
                act.wait_ge(st.centred[ln].sem, st.centred[ln].count(it, j + 1))
                act.activation(st.sq[:, j, :, :], st.cen[:, j, :, :], ACT.Square).then_inc(st.squared[ln].sem, 1)

            def attention(it, st, layer, stage, first_ln, i, phase):
                def copy_g(j):
                    n = layer * PAIRS + j
                    act.wait_ge(st.g_ready.sem, st.g_ready.count(it, n + 1))
                    act.copy(st.gT[:, j % 2, :], st.bank_g[:, :]).then_inc(st.g_copied.sem, 1)

                def copy_v(j):
                    n = layer * PAIRS + j
                    act.wait_ge(st.v_ready.sem, st.v_ready.count(it, n + 1))
                    act.copy(st.val[0:HALF, j, :, :], st.bank_g[0:HALF, 0:4 * AUG].rearrange("p (t e) -> p t e", t=4))\
                       .then_inc(st.v_copied.sem, 1)

                def exponent(k):
                    act.wait_ge(st.shifted.sem, st.shifted.count(it, layer * GROUP + k + 1))
                    act.activation(st.prob[:, k % 4, :, :], st.prob[:, k % 4, :, :], ACT.Exp).then_inc(st.exp_done.sem, 1)

                def copy_probs(k):
                    act.wait_ge(st.probs_turned.sem, st.probs_turned.count(it, layer * GROUP + k + 1))
                    act.copy(st.probT[0:HALF, k % 2, :, :], st.bank_p[0:HALF, :].rearrange("p (h s) -> p h s", h=2))\
                       .then_inc(st.probT_ready.sem, 1)

                if phase == 0 and 0 <= i - 3 < GROUP:
                    exponent(i - 3)
                if phase == 0 and pair_at(i, 8) is not None:
                    square(it, st, first_ln, pair_at(i, 8))
                if phase == 1 and pair_at(i, 2) is not None:
                    copy_v(pair_at(i, 2))
                if phase == 2 and pair_at(i, 1) is not None:
                    copy_g(pair_at(i, 1))
                if phase == 3 and 0 <= i - 4 < GROUP:
                    copy_probs(i - 4)
                if phase == 3 and stage is not None and pair_at(i, 0) is not None:
                    copy_x(it, st, stage, pair_at(i, 0), st.xT)

            def ffn(it, i, phase):
                if phase == 1 and pair_at(i, 0, 1) is not None:
                    j = i
                    for c in range(2):
                        act.wait_ge(hid_ready.sem, hid_ready.count(it, 2 * j + c + 1))
                        act.activation(hid[:, j % 2, c, :], B.bank[c][:, :], ACT.Gelu_apprx_tanh).then_inc(gelu_done.sem, 1)
                if phase == 3 and pair_at(i, 1, 1) is not None:
                    j = i - 1
                    act.wait_ge(B.out_ready.sem, B.out_ready.count(it, O_FFN * PAIRS + j + 1))
                    act.copy(pairwise(y[:, j, :, :]), B.outputs(FEAT)).then_inc(B.out_read.sem, 1)
                if phase == 0 and pair_at(i, 5, 1) is not None:
                    square(it, B, LN_FFN, i - 5)

            def moe(it, i, phase):
                if phase == 1 and pair_at(i, 2) is not None:
                    j = pair_at(i, 2)
                    act.wait_ge(cat_turned.sem, cat_turned.count(it, j + 1))
                    act.copy(catT[0:CAT, j % 3, :], B.bank_g[0:CAT, :]).then_inc(catT_ready.sem, 1)
                for half in range(2):
                    j = pair_at(i, 3 + half)
                    if phase == 2 and j is not None:
                        act.wait_ge(ehid_ready.sem, ehid_ready.count(it, 4 * j + 2 * half + 1))
                        act.activation(ehid[:, j % 2, 2 * half, :], B.bank[0][:, :], ACT.Relu).then_inc(relu_act.sem, 1)
                if phase == 3 and pair_at(i, 0) is not None:
                    copy_x(it, B, T_MOE, pair_at(i, 0), B.xT)
                if phase == 0 and pair_at(i, 7) is not None:
                    square(it, B, LN_MOE, pair_at(i, 7))

            def half_a(it, i, phase):
                if phase == 0 and i == AT_CONV:
                    for c in range(CHANNELS):
                        act.wait_ge(conv_ready.sem, conv_ready.count(it, c + 1))
                        act.activation(featT[0:FEAT, :, c * PER_CHANNEL:(c + 1) * PER_CHANNEL],
                                       A.bank[c][0:FEAT, :].rearrange("p (b j) -> p b j", b=GROUP),
                                       ACT.Identity, bias=P("convb", c, c + 1)).then_inc(feat_ready.sem, 1)
                attention(it, A, 0, None, LN_IN, i - AT_ATT0, phase)
                attention(it, A, 1, 0, LN_ATT, i - AT_ATT1, phase)
                if phase == 0 and pair_at(i, AT_ATT1 + 11) is not None:
                    square(it, A, LN_B, pair_at(i, AT_ATT1 + 11))
                if phase == 3 and pair_at(i, AT_ROUTER) is not None:
                    copy_x(it, A, T_FFN, pair_at(i, AT_ROUTER), h2T)

            def half_b(it, i, phase):
                ffn(it, i - AT_FFN, phase)
                attention(it, B, 0, T_ATT, LN_D, i - AT_ATT2, phase)
                moe(it, i - AT_MOE, phase)

            act.wait_ge(params_in.sem, 16)
            run(act, half_a, half_b)

        @block.vector
        def _(dve):
            dve.memset(neg_half[:, :], -0.5)
            dve.wait_ge(params_in.sem, 16)
            qkv_cols = par[0:FEAT, START["wqB"]:START["wqB"] + 3 * FEAT].rearrange("p (n c) -> p n c", n=3)
            dve.tensor_tensor(fold_tmp[:, :, :], qkv_cols, row(P("b1"), 3), ALU.mult).then_inc(folded_dve.sem, 1)
            dve.wait_ge(folded_dve.sem, 1)
            dve.tensor_reduce(qkv_sum[:, :], fold_tmp[:, :, :], AX_X, ALU.add).then_inc(folded_dve.sem, 1)
            dve.wait_ge(folded_dve.sem, 2)
            dve.tensor_tensor(qkv_fold[:, :, 0:FEAT], qkv_cols, row(P("g1"), 3), ALU.mult)
            dve.memset(qkv_fold[:, :, AUG:ROWS], 0.0)
            dve.tensor_tensor(qkv_fold[:, :, FEAT:AUG], qkv_sum[:, :].unsqueeze(2), P("qkvb").unsqueeze(2), ALU.add)\
               .then_inc(folded_dve.sem, 1)
            for c in range(CHANNELS):
                for a in range(2):
                    dve.tensor_scalar(conv_lhs[:, c, a, :], P("eye2"), P("convw", 2 * c + a, 2 * c + a + 1), None, ALU.mult)
            for t in (featT, h2T, A.xT, B.xT):
                dve.tensor_copy(t[:, :, :], row(P("xinit"), GROUP))
            root = 1.0 / float(FEAT) ** 0.5
            dve.wait_ge(folded_pe.sem, 1)
            dve.tensor_scalar(a_mat[0][:, :], A.bank[0][:, 0:ROWS], root, None, ALU.mult)
            dve.scalar_tensor_tensor(a_mat[2][:, :], A.bank[1][:, 0:ROWS], root, P("betaD"), ALU.mult, ALU.add)
            dve.tensor_copy(v_mat[0][:, FEAT:AUG], P("vaddA", FEAT, AUG))
            dve.tensor_tensor(v_mat[0][:, 0:FEAT], A.bank[2][:, 0:FEAT], P("vaddA", 0, FEAT), ALU.add)
            dve.wait_ge(folded_pe.sem, 2)
            dve.tensor_copy(a_mat[1][:, :], B.bank[0][:, 0:ROWS])
            dve.tensor_copy(v_mat[1][:, FEAT:AUG], P("vaddB", FEAT, AUG))
            dve.scalar_tensor_tensor(v_mat[1][:, 0:FEAT], B.bank[1][:, 0:FEAT], P("scaleB"),
                                     P("vaddB", 0, FEAT), ALU.mult, ALU.add).then_inc(setup_done.sem, 1)

            def centre(it, st, ln, j, src, sem, need):
                n = ln * PAIRS + j
                dve.wait_ge(sem, need)
                dve.tensor_reduce(st.mean[:, j, :], src, AX_X, ALU.add).then_inc(st.summed[ln].sem, 1)
                dve.wait_ge(st.summed[ln].sem, st.summed[ln].count(it, j + 1))
                dve.scalar_tensor_tensor(st.cen[:, j, :, :], bc(st.mean[:, j, :], FEAT), -1.0 / FEAT, src,
                                         ALU.mult, ALU.add).then_inc(st.centred[ln].sem, 1)

            def variance(it, st, ln, j):
                dve.wait_ge(st.squared[ln].sem, st.squared[ln].count(it, j + 1))
                dve.tensor_reduce(st.var[:, j, :], st.sq[:, j, :, :], AX_X, ALU.add).then_inc(st.var_ready[ln].sem, 1)

            def attention(it, st, layer, out_at, first_ln, biases, dst, i, phase):
                def soften(k):
                    n = layer * GROUP + k
                    s = st.bank_s[0:HALF, :].rearrange("p (h t) -> p h t", h=2)
                    prob = st.prob[:, k % 4, :, :]
                    dve.wait_ge(st.scores_ready.sem, st.scores_ready.count(it, n + 1))
                    if biases:
                        dve.tensor_tensor(prob, s, P("bias").rearrange("p (h t) -> p h t", h=2), ALU.add)\
                           .then_inc(biased.sem, 1)
                        dve.wait_ge(biased.sem, biased.count(it, k + 1))
                        s = prob
                    dve.tensor_reduce(st.peak[:, k % 4, :], s, AX_X, ALU.max).then_inc(st.peaked.sem, 1)
                    dve.wait_ge(st.peaked.sem, st.peaked.count(it, n + 1))
                    dve.tensor_tensor(prob, s, bc(st.peak[:, k % 4, :], TOKENS), ALU.subtract).then_inc(st.shifted.sem, 1)

                def divide(j):
                    n = layer * PAIRS + j
                    o = st.outputs(AUG)
                    sums = st.rsum[:, j, :].rearrange("p (b h) -> p b h", b=2)
                    dve.wait_ge(st.out_ready.sem, st.out_ready.count(it, out_at * PAIRS + j + 1))
                    dve.reciprocal(sums, o[:, :, :, FEAT]).then_inc(st.sum_inverted.sem, 1)
                    dve.wait_ge(st.sum_inverted.sem, st.sum_inverted.count(it, n + 1))
                    dve.tensor_tensor(pairwise(dst[:, j, :, :]), o[:, :, :, 0:FEAT],
                                      sums.unsqueeze(3).to_broadcast([HALF, 2, 2, FEAT]), ALU.mult)\
                       .then_inc(st.out_read.sem, 1)

                def centre_output(j):
                    done = st.out_read.count(it, out_at * PAIRS + j + 1)
                    if dst is not B.u:
                        centre(it, st, first_ln, j, dst[:, j, :, :], st.out_read.sem, done)
                    else:
                        dve.wait_ge(st.out_read.sem, done)
                        dve.tensor_tensor(B.u[:, j, :, :], B.u[:, j, :, :], h3[:, j, :, :], ALU.add).then_inc(att_ready.sem, 1)
                        centre(it, st, first_ln, j, B.u[:, j, :, :], att_ready.sem, att_ready.count(it, j + 1))

                if phase == 0 and pair_at(i, 7) is not None:
                    divide(pair_at(i, 7))
                if phase == 1 and 0 <= i - 2 < GROUP:
                    soften(i - 2)
                if phase == 2 and pair_at(i, 7) is not None:
                    centre_output(pair_at(i, 7))
                if phase == 2 and pair_at(i, 8) is not None:
                    variance(it, st, first_ln, pair_at(i, 8))

            def then_top(it, n, ins):
                ins.then_inc(top_step.sem, 1)
                dve.wait_ge(top_step.sem, top_step.count(it, n + 1))
                hold(dve, dve_gate)

            def ffn(it, i, phase):
                def round_of_8(r):
                    then_top(it, 2 * r + 1, dve.max(top8[:, :], work[:, :]))
                    then_top(it, 2 * r + 2, dve.match_replace(work[:, :], top8[:, :], work[:, :], LOWEST))

                if phase == 3 and i == 0:
                    dve.wait_ge(w_turned.sem, w_turned.count(it, 1))
                    dve.tensor_copy(work[:, :], B.bank_g[0:GROUP, 32:32 + TOKENS])
                    then_top(it, 0, dve.tensor_copy(wrow[:, :], B.bank_g[0:GROUP, 32:32 + TOKENS]))
                    for r in range(0, 2):
                        round_of_8(r)
                if phase == 3 and i == 1:
                    for r in range(2, 5):
                        round_of_8(r)
                if phase == 3 and i == 2:
                    for r in range(5, TOPK // 8):
                        round_of_8(r)
                    n = 2 * (TOPK // 8) + 1
                    then_top(it, n, dve.max(top8[:, :], work[:, :]))
                    then_top(it, n + 1, dve.memset(top8[:, TOPK % 8:8], LOWEST))
                    then_top(it, n + 2, dve.match_replace(work[:, :], top8[:, :], work[:, :], LOWEST))
                    then_top(it, n + 3, dve.tensor_tensor(work[:, :], work[:, :], wrow[:, :], ALU.not_equal))
                    then_top(it, n + 4, dve.tensor_tensor(wmrow[:, :], work[:, :], wrow[:, :], ALU.mult))
                if phase == 1 and i == 3:
                    dve.wait_ge(wm_turned.sem, wm_turned.count(it, 1))
                    dve.tensor_copy(wm[:, :, :], B.bank_g[0:HALF, 192:192 + 2 * GROUP].rearrange("p (h b) -> p h b", h=2))\
                       .then_inc(wm_ready.sem, 1)
                if phase == 2 and pair_at(i, 4, 1) is not None:
                    j = i - 4
                    dve.wait_ge(y_scaled.sem, y_scaled.count(it, j + 1))
                    dve.scalar_tensor_tensor(B.u[:, j, :, :], h2[:, j, :, :], 2.0, y[:, j, :, :], ALU.mult, ALU.add)\
                       .then_inc(u_ready.sem, 1)
                    centre(it, B, LN_FFN, j, B.u[:, j, :, :], u_ready.sem, u_ready.count(it, j + 1))
                if phase == 1 and pair_at(i, 5, 1) is not None:
                    variance(it, B, LN_FFN, i - 5)

            def moe(it, i, phase):
                def pick(j):
                    lg = B.bank_g[0:HALF, 0:4 * EXPERTS].rearrange("p (t e) -> p t e", t=4)
                    dve.wait_ge(logits_ready.sem, logits_ready.count(it, j + 1))
                    dve.tensor_reduce(lmax[:, j, 0, :], lg, AX_X, ALU.max).then_inc(route.sem, 1)
                    dve.wait_ge(route.sem, route.count(it, 4 * j + 1))
                    dve.tensor_tensor(hit[:, j, :, :], lg, bc(lmax[:, j, 0, :], EXPERTS), ALU.is_equal).then_inc(route.sem, 1)
                    dve.wait_ge(route.sem, route.count(it, 4 * j + 2))
                    dve.tensor_tensor(rank[:, j, :, :], hit[:, j, :, :], row(P("desc"), 4), ALU.mult).then_inc(route.sem, 1)
                    dve.wait_ge(route.sem, route.count(it, 4 * j + 3))
                    dve.tensor_reduce(lmax[:, j, 1, :], rank[:, j, :, :], AX_X, ALU.max).then_inc(route.sem, 1)
                    dve.wait_ge(route.sem, route.count(it, 4 * j + 4))
                    dve.tensor_tensor(cat[:, j, :, FEAT:CAT], rank[:, j, :, :], bc(lmax[:, j, 1, :], EXPERTS), ALU.is_equal)\
                       .then_inc(routed.sem, 1)

                if phase == 2 and pair_at(i, 1) is not None:
                    pick(pair_at(i, 1))
                for half in range(2):
                    j = pair_at(i, 3 + half)
                    if phase == 2 and j is not None:
                        dve.wait_ge(ehid_ready.sem, ehid_ready.count(it, 4 * j + 2 * half + 2))
                        dve.tensor_scalar(ehid[:, j % 2, 2 * half + 1, :], B.bank[1][:, :], 0.0, None, ALU.max)\
                           .then_inc(relu_dve.sem, 1)
                j = pair_at(i, 6)
                if phase == 2 and j is not None:
                    dve.wait_ge(B.out_ready.sem, B.out_ready.count(it, O_MOE * PAIRS + j + 1))
                    dve.scalar_tensor_tensor(pairwise(B.u[:, j, :, :]), B.outputs(FEAT), 0.0,
                                             pairwise(cat[:, j, :, 0:FEAT]), ALU.max, ALU.add).then_inc(B.out_read.sem, 1)
                    centre(it, B, LN_MOE, j, B.u[:, j, :, :], B.out_read.sem, B.out_read.count(it, O_MOE * PAIRS + j + 1))
                if phase == 1 and pair_at(i, 7) is not None:
                    variance(it, B, LN_MOE, pair_at(i, 7))

            def half_a(it, i, phase):
                attention(it, A, 0, 0, LN_IN, False, h1, i - AT_ATT0, phase)
                attention(it, A, 1, 1, LN_ATT, True, att, i - AT_ATT1, phase)
                j = pair_at(i, AT_ATT1 + 10)
                if phase == 2 and j is not None:
                    centre(it, A, LN_B, j, A.u[:, j, :, :], gained.sem, gained.count(it, 2 * j + 2))
                j = pair_at(i, AT_ATT1 + 11)
                if phase == 1 and j is not None:
                    variance(it, A, LN_B, j)
                if phase == 3 and i == AT_ROUTER + 7:
                    dve.wait_ge(w_ready.sem, w_ready.count(it, 1))
                    dve.tensor_copy(wcol[:, :, :], A.bank_o[0:HALF, 0:2 * GROUP].rearrange("p (h b) -> p h b", h=2))\
                       .then_inc(w_copied.sem, 1)

            def half_b(it, i, phase):
                ffn(it, i - AT_FFN, phase)
                attention(it, B, 0, O_ATT, LN_D, False, B.u, i - AT_ATT2, phase)
                moe(it, i - AT_MOE, phase)

            run(dve, half_a, half_b)

        @block.gpsimd
        def _(pool):
            for last in stored:
                pool.sem_inc(last.sem, last.head)
            for t in (A.probT, B.probT, A.val, B.val, catT):
                fill = pool.memset(t[:], 0.0)
            fill.then_inc(padded.sem, 1)
            pool.wait_ge(setup_done.sem, 1)

            def scale(it, st, ln, j, dst):
                n = ln * PAIRS + j
                pool.wait_ge(st.var_ready[ln].sem, st.var_ready[ln].count(it, j + 1))
                hold(pool, pool_gate)
                pool.tensor_scalar(st.rstd[:, j, :], st.var[:, j, :], 1.0 / FEAT, EPS, ALU.mult, ALU.add)\
                    .then_inc(st.var_eps[ln].sem, 1)
                pool.wait_ge(st.var_eps[ln].sem, st.var_eps[ln].count(it, j + 1))
                pool.tensor_tensor(st.rstd[:, j, :], st.rstd[:, j, :], neg_half[:, :], ALU.pow).then_inc(st.rstd_ready[ln].sem, 1)
                pool.wait_ge(st.rstd_ready[ln].sem, st.rstd_ready[ln].count(it, j + 1))
                pool.tensor_tensor(dst, st.cen[:, j, :, :], bc(st.rstd[:, j, :], FEAT), ALU.mult).then_inc(st.normed[ln].sem, 1)

            def half_a(it, i, phase):
                if phase:
                    return
                j = pair_at(i, AT_ATT0 + 8)
                if j is not None:
                    scale(it, A, LN_IN, j, xn[:, j, :, :])
                    pool.tensor_tensor(resid[:, j, :, :], h1[:, j, :, :], row(P("b2"), 4), ALU.add).then_inc(res_ready.sem, 1)
                j = pair_at(i, AT_ATT1 + 8)
                if j is not None:
                    scale(it, A, LN_ATT, j, on[:, j, :, :])
                    pool.wait_ge(A.normed[LN_ATT].sem, A.normed[LN_ATT].count(it, j + 1))
                    pool.tensor_tensor(on[:, j, :, :], on[:, j, :, :], row(P("g2"), 4), ALU.mult).then_inc(gained.sem, 1)
                    pool.wait_ge(gained.sem, gained.count(it, 2 * j + 1))
                    pool.wait_ge(res_ready.sem, res_ready.count(it, j + 1))
                    pool.tensor_tensor(A.u[:, j, :, :], on[:, j, :, :], resid[:, j, :, :], ALU.add).then_inc(gained.sem, 1)
                j = pair_at(i, AT_ATT1 + 11)
                if j is not None:
                    if it.ahead:
                        pool.wait_ge(u_ready.sem, u_ready.count(When(it.reg), j + 1))
                    scale(it, A, LN_B, j, h2[:, j, :, :])

            def half_b(it, i, phase):
                if phase:
                    return
                if pair_at(i, AT_FFN + 2, 1) is not None:
                    j = i - AT_FFN - 2
                    pool.wait_ge(B.out_read.sem, B.out_read.count(it, O_FFN * PAIRS + j + 1))
                    pool.tensor_tensor(y[:, j, :, :], y[:, j, :, :], row(P("fb2"), 4), ALU.add).then_inc(y_biased.sem, 1)
                if pair_at(i, AT_FFN + 3, 1) is not None:
                    j = i - AT_FFN - 3
                    if j == 0:
                        pool.wait_ge(wm_ready.sem, wm_ready.count(it, 1))
                    pool.wait_ge(y_biased.sem, y_biased.count(it, j + 1))
                    w = wm[:, :, 2 * j:2 * j + 2].rearrange("p h b -> p b h").unsqueeze(3).to_broadcast([HALF, 2, 2, FEAT])
                    pool.tensor_tensor(pairwise(y[:, j, :, :]), pairwise(y[:, j, :, :]), w, ALU.mult).then_inc(y_scaled.sem, 1)
                if pair_at(i, AT_FFN + 5, 1) is not None:
                    scale(it, B, LN_FFN, i - AT_FFN - 5, h3[:, i - AT_FFN - 5, :, :])
                j = pair_at(i, AT_ATT2 + 8)
                if j is not None:
                    scale(it, B, LN_D, j, cat[:, j, :, 0:FEAT])
                j = pair_at(i, AT_MOE + 7)
                if j is not None:
                    pool.wait_ge(stored[j].sem, stored[j].count(it, 0))
                    scale(it, B, LN_MOE, j, res[:, j, :, :])

            run(pool, half_a, half_b)


def _lay_out(inputs):
    f = {k: np.ascontiguousarray(np.asarray(v), dtype=np.float32) for k, v in inputs.items()}
    x = f["x"].reshape(IMAGES, 48, 2, 48, 2).transpose(2, 4, 0, 1, 3)
    x = x.reshape(2, 2, IMAGES, PER_CHANNEL, FEAT).transpose(1, 4, 0, 2, 3)
    pixels = np.ascontiguousarray(x).reshape(2 * FEAT, 2, IMAGES, PER_CHANNEL)

    par = np.zeros((128, PARAM_COLS), np.float32)

    def put(name, array, row=0, col=0):
        a = np.asarray(array, np.float32)
        c = START[name] + col
        par[row:row + a.shape[0], c:c + a.shape[1]] = a

    def rep(vector, rows):
        return np.broadcast_to(vector.reshape(1, -1), (rows, vector.size))

    put("ident", np.eye(128))
    put("eye2", np.eye(FEAT))
    put("eye2", np.eye(FEAT), row=FEAT)
    cw = f["L0_tok_conv_w"].reshape(CHANNELS, 2, 2)
    for b in range(2):
        put("convw", rep(cw[:, :, b], FEAT), row=b * FEAT)
    put("convb", rep(f["L0_tok_conv_b"], FEAT))
    pos = np.arange(TOKENS, dtype=np.float64)
    put("xinit", np.ones((1, TOKENS)), row=ONE)
    for n, period in enumerate(SCALES):
        put("xinit", np.stack([np.cos(2 * np.pi * pos / period), np.sin(2 * np.pi * pos / period)]), row=AUG + 2 * n)
    for name, w, b in (("wqA", "L0_tok_wq", "L0_tok_bq"), ("wkA", "L0_tok_wk", "L0_tok_bk"), ("wvA", "L0_tok_wv", "L0_tok_bv"),
                       ("wqD", "L1_attn_Wq", "L1_attn_bq"), ("wkD", "L1_attn_Wk", "L1_attn_bk")):
        put(name, f[w])
        put(name, f[b][:, None], col=FEAT)
    put("woA", f["L0_tok_wo"].T)
    put("vaddA", f["L0_tok_bo"][None], row=ONE)
    put("vaddA", np.ones((1, 1)), row=ONE, col=FEAT)
    qkv = f["L0_attn_qkv_w"].T
    for n, name in enumerate(("wqB", "wkB", "wvB")):
        put(name, qkv[n * FEAT:(n + 1) * FEAT])
        put("qkvb", f["L0_attn_qkv_b"][n * FEAT:(n + 1) * FEAT, None], col=n)
    put("g1", rep(f["L0_attn_ln1_g"], FEAT))
    put("b1", rep(f["L0_attn_ln1_b"], FEAT))
    put("projB", f["L0_attn_proj_w"])
    put("scaleB", rep(f["L0_attn_scale"].reshape(1), 128))
    put("vaddB", f["L0_attn_proj_b"][None], row=ONE)
    put("vaddB", np.ones((1, 1)), row=ONE, col=FEAT)
    put("g2", rep(f["L0_attn_ln2_g"], HALF))
    put("b2", rep(f["L0_attn_ln2_b"], HALF))
    table = f["L0_attn_bias_table"]
    key = np.arange(TOKENS)
    for h in range(2):
        query = h * HALF + np.arange(HALF)
        put("bias", table[key[None, :] - query[:, None] + TOKENS - 1], col=h * TOKENS)
    put("wr", f["L0_ffn_wr"])
    put("wr", f["L0_ffn_br"][None], row=ONE)
    put("w1", f["L0_ffn_w1"])
    put("w1", f["L0_ffn_b1"][None], row=ONE)
    for c in range(2):
        put("w2", f["L0_ffn_w2"][c * 128:(c + 1) * 128], col=c * FEAT)
    put("fb2", rep(f["L0_ffn_b2"], HALF))
    for n in range(2):
        for r in range(2):
            put("betaD", f["L1_attn_beta"][n].reshape(1, 1), row=AUG + 2 * n + r, col=AUG + 2 * n + r)
    put("vD", f["L1_attn_Wv"].T)
    put("vD", f["L1_attn_bv"][None], row=ONE)
    put("vD", np.ones((1, 1)), row=ONE, col=FEAT)
    put("router", f["L1_ffn_router_w"].T)
    put("router", f["L1_ffn_router_b"][None], row=ONE)
    put("ew1", f["L1_ffn_W1"].transpose(1, 0, 2).reshape(FEAT, MOE_H))
    put("ew1", np.full((EXPERTS, MOE_H), OFF), row=FEAT)
    for e in range(EXPERTS):
        put("ew1", f["L1_ffn_b1"][e][None], row=FEAT + e, col=e * HIDDEN)
    w2 = f["L1_ffn_W2"].reshape(MOE_H, FEAT)
    for c in range(4):
        put("ew2", w2[c * 128:(c + 1) * 128], col=c * FEAT)
    put("eb2", f["L1_ffn_b2"], row=FEAT)
    put("desc", rep(np.arange(EXPERTS, 0, -1), HALF))
    return pixels, par


def kernel(**inputs):
    import concourse.bacc as bacc
    from concourse.bass_utils import run_bass_kernel_spmd

    pixels, par = _lay_out(inputs)
    nc = bacc.Bacc("TRN2", target_bir_lowering=False, num_devices=1)
    pixels_dram = nc.dram_tensor("pixels", pixels.shape, F32, kind="ExternalInput").ap()
    params_dram = nc.dram_tensor("params", par.shape, F32, kind="ExternalInput").ap()
    out_dram = nc.dram_tensor("out", (IMAGES, TOKENS, FEAT), F32, kind="ExternalOutput").ap()
    build(nc, pixels_dram, params_dram, out_dram)
    r = run_bass_kernel_spmd(nc, [{"pixels": pixels, "params": par}], core_ids=[0])
    return r.results[0]["out"]
```

```python
from contextlib import ExitStack

import concourse.bass as bass
from concourse import mybir
import numpy as np

F32 = mybir.dt.float32
ALU = mybir.AluOpType
ACT = mybir.ActivationFunctionType
AX_X = mybir.AxisListType.X

IMAGES, TOKENS, FEAT = 64, 144, 64
HALF = TOKENS // 2
GROUP = 8
ITERS = IMAGES // GROUP
PAIRS = GROUP // 2
PAIR_TOKENS = 2 * TOKENS
CHANNELS = 4
CONV_BANKS = CHANNELS // 2
PER_CHANNEL = TOKENS // CHANNELS
ONE = FEAT
AUG = FEAT + 1
SCALES = (24.0, 720.0)
AUGC = AUG + 2 * len(SCALES)
ROWS = 128
EXPERTS, HIDDEN = 32, 16
MOE_H = EXPERTS * HIDDEN
HOT = ROWS - EXPERTS
FFN_H = 4 * FEAT
TOPK = TOKENS // 2 - 1
OFF = -1.0e30
LOWEST = -3.4028234663852886e38
EPS = 1e-5

SECTIONS = dict(
    eye2=(128, FEAT), convw=(128, 2 * CHANNELS), convb=(128, CHANNELS), xinit=(ROWS, TOKENS),
    wqA=(FEAT, ROWS), wkA=(FEAT, ROWS), wvA=(FEAT, ROWS), woA=(FEAT, FEAT), vaddA=(ROWS, AUG),
    wqB=(FEAT, FEAT), wkB=(FEAT, FEAT), wvB=(FEAT, FEAT), qkvb=(FEAT, 3), g1=(FEAT, FEAT), b1=(FEAT, FEAT),
    projB=(FEAT, FEAT), scaleB=(128, 1), vaddB=(ROWS, AUG),
    wqD=(FEAT, ROWS), wkD=(FEAT, ROWS), betaD=(ROWS, ROWS), ident=(128, 128),
    g2=(HALF, FEAT), b2=(HALF, FEAT), bias=(HALF, PAIR_TOKENS),
    wr=(ROWS, 1), w1=(ROWS, FFN_H), w2=(128, 2 * FEAT), fb2=(HALF, FEAT), vD=(ROWS, AUG),
    router=(ROWS, EXPERTS), ew1=(ROWS, MOE_H), ew2=(128, 4 * FEAT), eb2=(ROWS, FEAT), desc=(HALF, EXPERTS),
)
START = {}
_at = 0
for _name, (_rows, _cols) in SECTIONS.items():
    START[_name] = _at
    _at += _cols
PARAM_COLS = _at
FOLD_COLS = START["wqA"]
LAYER_COLS = START["ident"]


class When:

    def __init__(self, reg, ahead=0):
        self.reg, self.ahead = reg, ahead


class Step:

    def __init__(self, sem, per, head):
        self.sem, self.per, self.head = sem, per, head

    def count(self, when, n):
        return when.reg * self.per + (when.ahead * self.per + n + self.head)


def build(nc, pixels, params, out):
    with ExitStack() as ctx:
        def sb(name, shape):
            return ctx.enter_context(nc.sbuf_tensor(name, shape, F32))

        def step(name, per, head=0):
            return Step(ctx.enter_context(nc.semaphore(name)), per, head)

        par = sb("par", [128, PARAM_COLS])

        def P(name, c0=0, c1=None):
            rows, cols = SECTIONS[name]
            return par[0:rows, START[name] + c0:START[name] + (cols if c1 is None else c1)]

        class Stream:

            def __init__(self, tag, layers, norms):
                self.xT = sb("xT" + tag, [ROWS, GROUP, TOKENS])
                self.gT = sb("gT" + tag, [ROWS, 2, PAIR_TOKENS])
                self.val = sb("val" + tag, [ROWS, 4, 4, AUG])
                self.prob = sb("prob" + tag, [HALF, 4, 2, TOKENS])
                self.probT = sb("probT" + tag, [ROWS, 2, 2, TOKENS])
                self.peak = sb("peak" + tag, [HALF, 4, 2])
                self.rsum = sb("rsum" + tag, [HALF, 4, 4])
                self.u = sb("u" + tag, [HALF, 4, 4, FEAT])
                self.cen = sb("cen" + tag, [HALF, 4, 4, FEAT])
                self.sq = sb("sq" + tag, [HALF, 4, 4, FEAT])
                self.mean = sb("mean" + tag, [HALF, 4, 4])
                self.var = sb("var" + tag, [HALF, 4, 4])
                self.rstd = sb("rstd" + tag, [HALF, 4, 4])
                banks = ctx.enter_context(nc.psum_tensor("banks" + tag, [128, 4, 512], F32))
                self.bank = [banks[:, b, 0:PAIR_TOKENS] for b in range(4)]
                self.bank_s, self.bank_p, self.bank_g, self.bank_o = self.bank

                def outputs(width):
                    return banks[0:HALF, 3, 0:4 * width].rearrange("p (b h e) -> p b h e", b=2, h=2)

                self.outputs = outputs
                turns, outs = (2, 2) if tag == "a" else (2, 3)
                self.turned = step("turned_" + tag, turns * PAIRS)
                self.x_ready = step("x_ready_" + tag, turns * PAIRS)
                self.g_ready = step("g_ready_" + tag, layers * PAIRS)
                self.g_copied = step("g_copied_" + tag, layers * PAIRS)
                self.v_ready = step("v_ready_" + tag, layers * PAIRS)
                self.v_copied = step("v_copied_" + tag, layers * PAIRS)
                self.scores_ready = step("scores_ready_" + tag, layers * GROUP)
                self.peaked = step("peaked_" + tag, layers * GROUP)
                self.exp_done = step("exp_done_" + tag, layers * GROUP)
                self.probs_turned = step("probs_turned_" + tag, layers * GROUP)
                self.probT_ready = step("probT_ready_" + tag, layers * GROUP)
                self.out_ready = step("out_ready_" + tag, outs * PAIRS)
                self.out_read = step("out_read_" + tag, outs * PAIRS, 1)
                self.sum_inverted = step("sum_inverted_" + tag, layers * PAIRS)
                self.summed = [step(f"summed_{tag}{n}", PAIRS) for n in range(norms)]
                self.centred = [step(f"centred_{tag}{n}", PAIRS) for n in range(norms)]
                self.squared = [step(f"squared_{tag}{n}", PAIRS) for n in range(norms)]
                self.var_ready = [step(f"var_ready_{tag}{n}", PAIRS) for n in range(norms)]
                self.var_eps = [step(f"var_eps_{tag}{n}", PAIRS) for n in range(norms)]
                self.rstd_ready = [step(f"rstd_ready_{tag}{n}", PAIRS) for n in range(norms)]
                self.normed = [step(f"normed_{tag}{n}", PAIRS) for n in range(norms)]

        LN_IN, LN_ATT, LN_B = range(3)
        LN_FFN, LN_D, LN_MOE = range(3)
        T_IN, T_FFN = range(2)
        T_ATT, T_MOE = range(2)
        O_FFN, O_ATT, O_MOE = range(3)
        A, B = Stream("a", 2, 3), Stream("b", 1, 3)

        conv_lhs = sb("conv_lhs", [128, CONV_BANKS, 2, 2 * FEAT])
        a_mat = [sb(f"a_mat{n}", [ROWS, ROWS]) for n in range(3)]
        v_mat = [sb(f"v_mat{n}", [ROWS, AUG]) for n in range(2)]
        qkv_fold = sb("qkv_fold", [FEAT, 3, ROWS])
        qkv_sum = sb("qkv_sum", [FEAT, 3])
        fold_tmp = sb("fold_tmp", [FEAT, 3, FEAT])
        neg_half = sb("neg_half", [HALF, 4])
        first_exp = sb("first_exp", [FEAT, 1])

        pix = sb("pix", [128, 2, GROUP, PER_CHANNEL])
        featT = sb("featT", [ROWS, GROUP, TOKENS])
        h2T = sb("h2T", [ROWS, GROUP, TOKENS])
        att = sb("att", [HALF, 4, 4, FEAT])
        h1 = sb("h1", [HALF, 4, 4, FEAT])
        h2 = sb("h2", [HALF, 4, 4, FEAT])
        h3 = sb("h3", [HALF, 4, 4, FEAT])
        xn = sb("xn", [HALF, 4, 4, FEAT])
        on = sb("on", [HALF, 4, 4, FEAT])
        y = sb("y", [HALF, 4, 4, FEAT])
        resid = sb("resid", [HALF, 4, 4, FEAT])
        res = sb("res", [HALF, 4, 4, FEAT])
        feat_d = sb("feat_d", [HALF, 4, 4, FEAT])
        one_hot = sb("one_hot", [HALF, 4, 4, EXPERTS])
        hid = sb("hid", [128, 2, 2, PAIR_TOKENS])
        wcol = sb("wcol", [HALF, 2, GROUP])
        wrow = sb("wrow", [GROUP, TOKENS])
        work = sb("work", [GROUP, TOKENS])
        top8 = sb("top8", [GROUP, 8])
        wmrow = sb("wmrow", [GROUP, TOKENS])
        wm = sb("wm", [HALF, 2, GROUP])
        lmax = sb("lmax", [HALF, 4, 2, 4])
        hit = sb("hit", [HALF, 4, 4, EXPERTS])
        rank = sb("rank", [HALF, 4, 4, EXPERTS])
        ehid = sb("ehid", [128, 2, 4, PAIR_TOKENS])

        conv_params_in = step("conv_params_in", 0)
        fold_params_in = step("fold_params_in", 0)
        layer_params_in = step("layer_params_in", 0)
        conv_set = step("conv_set", 0)
        folded_dve = step("folded_dve", 0)
        padded = step("padded", 0)
        folded_pe = step("folded_pe", 0)
        setup_done = step("setup_done", 0)
        pixels_in = step("pixels_in", 16)
        conv_ready = step("conv_ready", CONV_BANKS)
        feat_ready = step("feat_ready", CHANNELS)
        biased = step("biased", GROUP)
        att_ready = step("att_ready", PAIRS)
        u_ready = step("u_ready", PAIRS)
        gained = step("gained", 2 * PAIRS)
        res_ready = step("res_ready", PAIRS)
        w_ready = step("w_ready", 1)
        w_copied = step("w_copied", 1, head=1)
        w_turned = step("w_turned", 1)
        TOP_STEPS = 2 * (TOPK // 8) + 6
        top_step = step("top_step", TOP_STEPS)
        wm_turned = step("wm_turned", 1)
        wm_ready = step("wm_ready", 1)
        hid_ready = step("hid_ready", 2 * PAIRS)
        gelu_done = step("gelu_done", 2 * PAIRS)
        y_biased = step("y_biased", PAIRS)
        y_scaled = step("y_scaled", PAIRS)
        logits_ready = step("logits_ready", PAIRS)
        route = step("route", 4 * PAIRS)
        routed = step("routed", PAIRS)
        hot_turned = step("hot_turned", PAIRS)
        hot_ready = step("hot_ready", PAIRS)
        ehid_ready = step("ehid_ready", 4 * PAIRS)
        relu_act = step("relu_act", 2 * PAIRS)
        relu_dve = step("relu_dve", 2 * PAIRS)
        stored = [step(f"stored{j}", 16, head=16) for j in range(PAIRS)]
        pe_gate = step("pe_gate", 0)
        dve_gate = step("dve_gate", 0)
        pool_gate = step("pool_gate", 0)

        def hold(eng, gate):
            eng.sem_inc(gate.sem, 1)

        block = ctx.enter_context(nc.Block())

        def bc(ap2, n):
            return ap2.unsqueeze(2).to_broadcast([ap2.shape[0], ap2.shape[1], n])

        def row(ap2, n):
            return ap2.unsqueeze(1).to_broadcast([ap2.shape[0], n, ap2.shape[1]])

        def pairwise(ap3):
            return ap3.rearrange("p (b h) e -> p b h e", b=2)

        EARLY = 0
        CYCLE = 262
        PLACES = {
            "att0.g": (16, 16, PAIRS), "att0.copy_g": (18, 16, PAIRS), "att0.v": (22, 16, PAIRS),
            "att0.copy_v": (24, 16, PAIRS), "att0.scores": (22, 8, GROUP), "att0.peak": (24, 8, GROUP),
            "att0.exp": (26, 8, GROUP), "att0.turn_probs": (34, 8, GROUP), "att0.copy_probs": (35, 8, GROUP),
            "att0.weigh": (42, 8, GROUP), "att0.divide": (54, 16, PAIRS), "att0.centre": (57, 16, PAIRS),
            "att0.square": (60, 16, PAIRS), "att0.variance": (64, 16, PAIRS), "att0.norm": (62, 16, PAIRS),
            "att1.turn": (73, 16, PAIRS), "att1.copy_x": (74, 16, PAIRS), "att1.g": (78, 16, PAIRS),
            "att1.copy_g": (80, 16, PAIRS), "att1.v": (84, 16, PAIRS), "att1.copy_v": (83, 16, PAIRS),
            "att1.scores": (84, 8, GROUP), "att1.peak": (86, 8, GROUP), "att1.exp": (88, 8, GROUP),
            "att1.turn_probs": (97, 8, GROUP), "att1.copy_probs": (99, 8, GROUP), "att1.weigh": (104, 8, GROUP),
            "att1.divide": (115, 16, PAIRS), "att1.centre": (121, 16, PAIRS), "att1.square": (122, 16, PAIRS),
            "att1.variance": (126, 16, PAIRS), "att1.norm": (124, 16, PAIRS),
            "att2.turn": (52, 16, PAIRS), "att2.copy_x": (55, 16, PAIRS), "att2.g": (58, 16, PAIRS),
            "att2.copy_g": (59, 16, PAIRS), "att2.v": (64, 16, PAIRS), "att2.copy_v": (66, 16, PAIRS),
            "att2.scores": (64, 8, GROUP), "att2.peak": (66, 8, GROUP), "att2.exp": (68, 8, GROUP),
            "att2.turn_probs": (77, 8, GROUP), "att2.copy_probs": (79, 8, GROUP), "att2.weigh": (86, 8, GROUP),
            "att2.divide": (97, 16, PAIRS), "att2.centre": (101, 16, PAIRS), "att2.square": (106, 16, PAIRS),
            "att2.variance": (108, 16, PAIRS), "att2.norm": (106, 16, PAIRS),
            "conv.products": (4, 8, 1), "conv.bias": (9, 8, 1),
            "router.gain": (136, 16, PAIRS), "router.centre": (138, 16, PAIRS), "router.square": (142, 16, PAIRS),
            "router.variance": (144, 16, PAIRS), "router.norm": (148, 16, PAIRS), "router.turn": (158, 16, PAIRS),
            "router.copy_x": (165, 16, PAIRS), "router.weights": (167, 16, PAIRS), "router.copy_w": (211, 8, 1),
            "ffn.turn_w": (0, 8, 1), "ffn.hidden": (0, 8, PAIRS), "ffn.gelu": (2, 8, PAIRS), "ffn.second": (9, 8, PAIRS),
            "ffn.copy_y": (14, 8, PAIRS), "ffn.top_start": (6, 8, 1), "ffn.top_round": (15, 1, TOPK // 8),
            "ffn.top_end": (22, 8, 1), "ffn.turn_wm": (27, 8, 1), "ffn.copy_wm": (26, 8, 1), "ffn.bias": (18, 8, PAIRS),
            "ffn.weight": (24, 8, PAIRS), "ffn.centre": (36, 8, PAIRS), "ffn.square": (40, 8, PAIRS),
            "ffn.variance": (42, 8, PAIRS), "ffn.norm": (53, 8, PAIRS),
            "moe.turn": (119, 16, PAIRS), "moe.copy_x": (119, 16, PAIRS), "moe.logits": (124, 16, PAIRS),
            "moe.pick": (126, 16, PAIRS), "moe.turn_hot": (128, 16, PAIRS), "moe.copy_hot": (133, 16, PAIRS),
            "moe.hidden01": (140, 16, PAIRS), "moe.hidden23": (148, 16, PAIRS), "moe.relu01": (142, 16, PAIRS),
            "moe.relu23": (152, 16, PAIRS), "moe.second": (158, 16, PAIRS), "moe.centre": (163, 16, PAIRS),
            "moe.square": (172, 16, PAIRS), "moe.variance": (173, 16, PAIRS), "moe.norm": (171, 16, PAIRS),
        }
        CYCLE_ALONE = 248
        PLACES_ALONE = {
            "att0.g": (12, 16, PAIRS), "att0.copy_g": (14, 16, PAIRS), "att0.v": (19, 16, PAIRS),
            "att0.copy_v": (22, 16, PAIRS), "att0.scores": (19, 8, GROUP), "att0.peak": (21, 8, GROUP),
            "att0.exp": (23, 8, GROUP), "att0.turn_probs": (32, 8, GROUP), "att0.copy_probs": (34, 8, GROUP),
            "att0.weigh": (39, 8, GROUP), "att0.divide": (48, 16, PAIRS), "att0.centre": (51, 16, PAIRS),
            "att0.square": (59, 16, PAIRS), "att0.variance": (61, 16, PAIRS), "att0.norm": (61, 16, PAIRS),
            "att1.turn": (69, 16, PAIRS), "att1.copy_x": (72, 16, PAIRS), "att1.g": (74, 16, PAIRS),
            "att1.copy_g": (76, 16, PAIRS), "att1.v": (80, 16, PAIRS), "att1.copy_v": (83, 16, PAIRS),
            "att1.scores": (80, 8, GROUP), "att1.peak": (82, 8, GROUP), "att1.exp": (84, 8, GROUP),
            "att1.turn_probs": (94, 8, GROUP), "att1.copy_probs": (95, 8, GROUP), "att1.weigh": (100, 8, GROUP),
            "att1.divide": (111, 16, PAIRS), "att1.centre": (115, 16, PAIRS), "att1.square": (121, 16, PAIRS),
            "att1.variance": (123, 16, PAIRS), "att1.norm": (116, 16, PAIRS),
            "att2.turn": (49, 16, PAIRS), "att2.copy_x": (51, 16, PAIRS), "att2.g": (55, 16, PAIRS),
            "att2.copy_g": (56, 16, PAIRS), "att2.v": (61, 16, PAIRS), "att2.copy_v": (60, 16, PAIRS),
            "att2.scores": (61, 8, GROUP), "att2.peak": (63, 8, GROUP), "att2.exp": (65, 8, GROUP),
            "att2.turn_probs": (75, 8, GROUP), "att2.copy_probs": (76, 8, GROUP), "att2.weigh": (83, 8, GROUP),
            "att2.divide": (94, 16, PAIRS), "att2.centre": (95, 16, PAIRS), "att2.square": (103, 16, PAIRS),
            "att2.variance": (105, 16, PAIRS), "att2.norm": (103, 16, PAIRS),
            "conv.products": (0, 8, 1), "conv.bias": (8, 8, 1),
            "router.gain": (132, 16, PAIRS), "router.centre": (134, 16, PAIRS), "router.square": (138, 16, PAIRS),
            "router.variance": (139, 16, PAIRS), "router.norm": (142, 16, PAIRS), "router.turn": (174, 16, PAIRS),
            "router.copy_x": (157, 16, PAIRS), "router.weights": (181, 16, PAIRS), "router.copy_w": (231, 8, 1),
            "ffn.turn_w": (0, 8, 1), "ffn.hidden": (0, 8, PAIRS), "ffn.gelu": (3, 8, PAIRS), "ffn.second": (9, 8, PAIRS),
            "ffn.copy_y": (14, 8, PAIRS), "ffn.top_start": (6, 8, 1), "ffn.top_round": (11, 1, TOPK // 8),
            "ffn.top_end": (24, 8, 1), "ffn.turn_wm": (24, 8, 1), "ffn.copy_wm": (26, 8, 1), "ffn.bias": (20, 8, PAIRS),
            "ffn.weight": (24, 8, PAIRS), "ffn.centre": (32, 8, PAIRS), "ffn.square": (43, 8, PAIRS),
            "ffn.variance": (46, 8, PAIRS), "ffn.norm": (44, 8, PAIRS),
            "moe.turn": (116, 16, PAIRS), "moe.copy_x": (116, 16, PAIRS), "moe.logits": (119, 16, PAIRS),
            "moe.pick": (123, 16, PAIRS), "moe.turn_hot": (128, 16, PAIRS), "moe.copy_hot": (130, 16, PAIRS),
            "moe.hidden01": (137, 16, PAIRS), "moe.hidden23": (145, 16, PAIRS), "moe.relu01": (139, 16, PAIRS),
            "moe.relu23": (147, 16, PAIRS), "moe.second": (153, 16, PAIRS), "moe.centre": (155, 16, PAIRS),
            "moe.square": (164, 16, PAIRS), "moe.variance": (163, 16, PAIRS), "moe.norm": (163, 16, PAIRS),
        }

        def due(step_name, tick):
            at_tick, places = tick
            first, every, repeats = places[step_name]
            n, rest = divmod(at_tick - first, every)
            return n if rest == 0 and 0 <= n < repeats else None

        def run(eng, half_a, half_b):
            def at(tick, when_b, groups_a):
                ahead, tick_a = divmod(tick + EARLY, CYCLE)
                half_b(when_b, (tick, PLACES))
                if ahead < groups_a:
                    half_a(When(when_b.reg, when_b.ahead + 1 + ahead), (tick_a, PLACES))

            for tick in range(CYCLE_ALONE):
                half_a(When(0), (tick, PLACES_ALONE))
            for tick in range(EARLY):
                half_a(When(0, 1), (tick, PLACES))
            with eng.Fori(0, ITERS - 2) as g:
                for tick in range(CYCLE):
                    at(tick, When(g), 2)
            for tick in range(CYCLE):
                at(tick, When(0, ITERS - 2), 1)
            for tick in range(CYCLE_ALONE):
                half_b(When(0, ITERS - 1), (tick, PLACES_ALONE))

        @block.sync
        def _(sp):
            sp.dma_start(par[:, 0:FOLD_COLS], params[:, 0:FOLD_COLS]).then_inc(conv_params_in.sem, 16)
            sp.dma_start(par[:, FOLD_COLS:LAYER_COLS], params[:, FOLD_COLS:LAYER_COLS]).then_inc(fold_params_in.sem, 16)
            sp.dma_start(pix[:, :, :, :], pixels[:, :, 0:GROUP, :]).then_inc(pixels_in.sem, 16)

            def load_after(when, group):
                sp.wait_ge(conv_ready.sem, conv_ready.count(when, CONV_BANKS))
                sp.dma_start(pix[:, :, :, :], pixels[:, :, group, :]).then_inc(pixels_in.sem, 16)

            def store(when, group):
                for j in range(PAIRS):
                    sp.wait_ge(B.normed[LN_MOE].sem, B.normed[LN_MOE].count(when, j + 1))
                    dst = out[bass.ds(group * GROUP + 2 * j, 2), :, :].rearrange("b (h p) d -> p (b h) d", p=HALF)
                    sp.dma_start(dst, res[:, j, :, :]).then_inc(stored[j].sem, 16)

            sp.dma_start(par[:, LAYER_COLS:], params[:, LAYER_COLS:]).then_inc(layer_params_in.sem, 16)
            load_after(When(0), slice(GROUP, 2 * GROUP))
            with sp.Fori(0, ITERS - 2) as g:
                load_after(When(g, 1), bass.ds((g + 2) * GROUP, GROUP))
                store(When(g), g)
            store(When(0, ITERS - 2), ITERS - 2)
            store(When(0, ITERS - 1), ITERS - 1)
            for j in range(PAIRS):
                sp.wait_ge(stored[j].sem, 16 * (ITERS + 1))

        @block.tensor
        def _(pe):
            for head_start in (A.out_read, B.out_read, w_copied):
                pe.sem_inc(head_start.sem, head_start.head)
            pe.wait_ge(fold_params_in.sem, 16)
            pe.matmul(B.bank[0][:, 0:ROWS], P("wqA"), P("wkA"), start=True, stop=True)
            pe.matmul(B.bank[1][:, 0:ROWS], P("wqD"), P("wkD"), start=True, stop=True)
            pe.matmul(B.bank[2][:, 0:FEAT], P("wvA"), P("woA"), start=True, stop=True).then_inc(folded_pe.sem, 1)
            pe.wait_ge(folded_dve.sem, 3)
            pe.matmul(B.bank[3][:, 0:ROWS], qkv_fold[:, 0, :], qkv_fold[:, 1, :], start=True, stop=True)
            pe.matmul(B.bank[3][:, ROWS:ROWS + FEAT], qkv_fold[:, 2, :], P("projB"), start=True, stop=True)\
              .then_inc(folded_pe.sem, 1)
            pe.wait_ge(conv_set.sem, 1)

            def conv(it):
                pe.wait_ge(pixels_in.sem, pixels_in.count(it, 16))
                pe.wait_ge(w_copied.sem, w_copied.count(it, 0))
                for c in range(CONV_BANKS):
                    for a in range(2):
                        mm = pe.matmul(A.bank[c][:, :], conv_lhs[:, c, a, :], pix[:, a, :, :],
                                       start=a == 0, stop=a == 1)
                    mm.then_inc(conv_ready.sem, 1)
                if it.ahead == 0:
                    pe.wait_ge(setup_done.sem, 1)
                    pe.wait_ge(padded.sem, 1)
                    pe.wait_ge(layer_params_in.sem, 16)

            def turn(it, st, src, ln_of, ln, j, bank_free):
                pe.wait_ge(ln_of.normed[ln].sem, ln_of.normed[ln].count(it, j + 1))
                if bank_free is not None:
                    pe.wait_ge(bank_free[0].sem, bank_free[0].count(it, bank_free[1]))
                hold(pe, pe_gate)
                for b in range(2):
                    mm = pe.transpose(st.bank_g[:, b * HALF:(b + 1) * HALF], src[:, 2 * b:2 * b + 2, :],
                                      P("ident")[0:HALF, 0:HALF])
                mm.then_inc(st.turned.sem, 1)

            def attention(name, it, st, layer, out_at, src, am, vw, src_ready, turn_pair, tick):

                def project_g(j):
                    n = layer * PAIRS + j
                    sem, need = src_ready(j)
                    pe.wait_ge(sem, need)
                    if turn_pair is None and j >= 1:
                        pe.wait_ge(st.v_copied.sem, st.v_copied.count(it, n))
                    pe.matmul(st.bank_g[:, :], am[:, :], src[:, 2 * j:2 * j + 2, :],
                              start=True, stop=True).then_inc(st.g_ready.sem, 1)

                def project_v(j):
                    n = layer * PAIRS + j
                    pe.wait_ge(st.g_copied.sem, st.g_copied.count(it, n + 1))
                    for t in range(4):
                        mm = pe.matmul(st.bank_g[0:HALF, t * AUG:(t + 1) * AUG],
                                       src[:, 2 * j + t // 2, (t % 2) * HALF:(t % 2 + 1) * HALF], vw,
                                       start=True, stop=True)
                    mm.then_inc(st.v_ready.sem, 1)

                def scores(k):
                    n = layer * GROUP + k
                    pe.wait_ge(st.g_copied.sem, st.g_copied.count(it, layer * PAIRS + k // 2 + 1))
                    if am is a_mat[1] and k >= 1:
                        pe.wait_ge(biased.sem, biased.count(it, k))
                    elif st is B and k == 0:
                        pe.wait_ge(gelu_done.sem, gelu_done.count(it, 2 * PAIRS))
                    elif n >= 1:
                        pe.wait_ge(st.exp_done.sem, st.exp_done.count(it, n))
                    for h in range(2):
                        c = (k % 2) * TOKENS + h * HALF
                        mm = pe.matmul(st.bank_s[0:HALF, h * TOKENS:(h + 1) * TOKENS],
                                       st.gT[:, (k // 2) % 2, c:c + HALF], src[:, k, :], start=True, stop=True)
                    mm.then_inc(st.scores_ready.sem, 1)

                def turn_probs(k):
                    n = layer * GROUP + k
                    pe.wait_ge(st.exp_done.sem, st.exp_done.count(it, n + 1))
                    if n >= 1:
                        pe.wait_ge(st.probT_ready.sem, st.probT_ready.count(it, n))
                    for th in range(2):
                        for sh in range(2):
                            c = th * TOKENS + sh * HALF
                            mm = pe.transpose(st.bank_p[0:HALF, c:c + HALF],
                                              st.prob[:, k % 4, sh, th * HALF:(th + 1) * HALF], P("ident")[0:HALF, 0:HALF])
                    mm.then_inc(st.probs_turned.sem, 1)

                def weigh(k):
                    j = k // 2
                    pe.wait_ge(st.probT_ready.sem, st.probT_ready.count(it, layer * GROUP + k + 1))
                    pe.wait_ge(st.v_copied.sem, st.v_copied.count(it, layer * PAIRS + j + 1))
                    if k % 2 == 0:
                        pe.wait_ge(st.out_read.sem, st.out_read.count(it, out_at * PAIRS + j))
                    for sh in range(2):
                        for th in range(2):
                            mm = pe.matmul(st.outputs(AUG)[:, k % 2, sh, :],
                                           st.probT[:, k % 2, th, sh * HALF:(sh + 1) * HALF],
                                           st.val[:, j, (k % 2) * 2 + th, :], start=th == 0, stop=th == 1)
                    if k % 2 == 1:
                        mm.then_inc(st.out_ready.sem, 1)

                if (j := due(name + ".v", tick)) is not None:
                    project_v(j)
                if (k := due(name + ".scores", tick)) is not None:
                    scores(k)
                if (j := due(name + ".g", tick)) is not None:
                    project_g(j)
                if (k := due(name + ".turn_probs", tick)) is not None:
                    turn_probs(k)
                if (k := due(name + ".weigh", tick)) is not None:
                    weigh(k)
                if turn_pair is not None and (j := due(name + ".turn", tick)) is not None:
                    turn_pair(j)

            def router(it, tick):
                if (j := due("router.weights", tick)) is not None:
                    pe.wait_ge(A.x_ready.sem, A.x_ready.count(it, T_FFN * PAIRS + j + 1))
                    if j == 0:
                        pe.wait_ge(A.out_read.sem, A.out_read.count(it, 2 * PAIRS))
                    for t in range(4):
                        col = (t % 2) * GROUP + 2 * j + t // 2
                        mm = pe.matmul(A.bank_o[0:HALF, col:col + 1],
                                       h2T[:, 2 * j + t // 2, (t % 2) * HALF:(t % 2 + 1) * HALF], P("wr"),
                                       start=True, stop=True)
                    if j == PAIRS - 1:
                        mm.then_inc(w_ready.sem, 1)
                if (j := due("router.turn", tick)) is not None:
                    turn(it, A, h2[:, j, :, :], A, LN_B, j, (A.x_ready, T_FFN * PAIRS + j) if j else (A.v_copied, 2 * PAIRS))

            def ffn(it, tick):
                def hidden(j):
                    for c in range(2):
                        n = 2 * j + c
                        if n >= 2:
                            pe.wait_ge(gelu_done.sem, gelu_done.count(it, n - 1))
                        pe.matmul(B.bank[c][:, :], P("w1", 128 * c, 128 * (c + 1)),
                                  h2T[:, 2 * j:2 * j + 2, :], start=True, stop=True).then_inc(hid_ready.sem, 1)

                def second(j):
                    pe.wait_ge(gelu_done.sem, gelu_done.count(it, 2 * j + 2))
                    pe.wait_ge(B.out_read.sem, B.out_read.count(it, O_FFN * PAIRS + j))
                    for t in range(4):
                        for c in range(2):
                            mm = pe.matmul(B.outputs(FEAT)[:, t // 2, t % 2, :],
                                           hid[:, j % 2, c, t * HALF:(t + 1) * HALF], P("w2", c * FEAT, (c + 1) * FEAT),
                                           start=c == 0, stop=c == 1)
                    mm.then_inc(B.out_ready.sem, 1)

                if due("ffn.turn_w", tick) is not None:
                    pe.wait_ge(w_copied.sem, w_copied.count(it, 1))
                    for h in range(2):
                        mm = pe.transpose(B.bank_g[0:GROUP, 32 + h * HALF:32 + (h + 1) * HALF], wcol[:, h, :],
                                          P("ident")[0:HALF, 0:HALF])
                    mm.then_inc(w_turned.sem, 1)
                if (j := due("ffn.hidden", tick)) is not None:
                    hidden(j)
                if (j := due("ffn.second", tick)) is not None:
                    second(j)
                if due("ffn.turn_wm", tick) is not None:
                    pe.wait_ge(top_step.sem, top_step.count(it, TOP_STEPS))
                    hold(pe, pe_gate)
                    for h in range(2):
                        mm = pe.transpose(B.bank_g[0:HALF, 192 + h * GROUP:192 + (h + 1) * GROUP],
                                          wmrow[:, h * HALF:(h + 1) * HALF], P("ident")[0:GROUP, 0:GROUP])
                    mm.then_inc(wm_turned.sem, 1)

            def moe(it, tick):
                def logits(j):
                    pe.wait_ge(B.x_ready.sem, B.x_ready.count(it, T_MOE * PAIRS + j + 1))
                    for t in range(4):
                        mm = pe.matmul(B.bank_g[0:HALF, t * EXPERTS:(t + 1) * EXPERTS],
                                       B.xT[:, 2 * j + t // 2, (t % 2) * HALF:(t % 2 + 1) * HALF], P("router"),
                                       start=True, stop=True)
                    mm.then_inc(logits_ready.sem, 1)

                def turn_hot(j):
                    pe.wait_ge(routed.sem, routed.count(it, j + 1))
                    for t in range(4):
                        mm = pe.transpose(B.bank_g[0:EXPERTS, t * HALF:(t + 1) * HALF], one_hot[:, j, t, :],
                                          P("ident")[0:HALF, 0:HALF])
                    mm.then_inc(hot_turned.sem, 1)

                def hidden(j, c):
                    if c == 0:
                        pe.wait_ge(hot_ready.sem, hot_ready.count(it, j + 1))
                    if j == 0 and c == 1:
                        pe.wait_ge(B.probT_ready.sem, B.probT_ready.count(it, GROUP))
                    n = 2 * j + c // 2
                    if n >= 1:
                        done = relu_dve if c % 2 else relu_act
                        pe.wait_ge(done.sem, done.count(it, n))
                    pe.matmul(B.bank[c % 2][:, :], P("ew1", 128 * c, 128 * (c + 1)),
                              B.xT[:, 2 * j:2 * j + 2, :], start=True, stop=True).then_inc(ehid_ready.sem, 1)

                def second(j):
                    pe.wait_ge(relu_act.sem, relu_act.count(it, 2 * j + 2))
                    pe.wait_ge(relu_dve.sem, relu_dve.count(it, 2 * j + 2))
                    pe.wait_ge(B.out_read.sem, B.out_read.count(it, O_MOE * PAIRS + j))
                    for t in range(4):
                        for c in range(4):
                            pe.matmul(B.outputs(FEAT)[:, t // 2, t % 2, :],
                                      ehid[:, j % 2, c, t * HALF:(t + 1) * HALF], P("ew2", c * FEAT, (c + 1) * FEAT),
                                      start=c == 0, stop=False)
                        mm = pe.matmul(B.outputs(FEAT)[:, t // 2, t % 2, :],
                                       B.xT[HOT:ROWS, 2 * j + t // 2, (t % 2) * HALF:(t % 2 + 1) * HALF], P("eb2")[HOT:ROWS, :],
                                       start=False, stop=True)
                    mm.then_inc(B.out_ready.sem, 1)

                if (j := due("moe.logits", tick)) is not None:
                    logits(j)
                if (j := due("moe.turn_hot", tick)) is not None:
                    turn_hot(j)
                if (j := due("moe.hidden01", tick)) is not None:
                    hidden(j, 0)
                    hidden(j, 1)
                if (j := due("moe.hidden23", tick)) is not None:
                    hidden(j, 2)
                    hidden(j, 3)
                if (j := due("moe.second", tick)) is not None:
                    second(j)
                if (j := due("moe.turn", tick)) is not None:
                    turn(it, B, feat_d[:, j, :, :], B, LN_D, j, (hot_ready, j) if j else (B.v_copied, PAIRS))

            def half_a(it, tick):
                if due("conv.products", tick) is not None:
                    conv(it)
                attention("att0", it, A, 0, 0, featT, a_mat[0], v_mat[0][:, :],
                          lambda j: (feat_ready.sem, feat_ready.count(it, CHANNELS)), None, tick)
                attention("att1", it, A, 1, 1, A.xT, a_mat[1], v_mat[1][:, :],
                          lambda j: (A.x_ready.sem, A.x_ready.count(it, j + 1)),
                          lambda j: turn(it, A, xn[:, j, :, :], A, LN_IN, j, (A.v_copied, PAIRS + j)), tick)
                router(it, tick)

            def half_b(it, tick):
                ffn(it, tick)
                attention("att2", it, B, 0, O_ATT, B.xT, a_mat[2], P("vD"),
                          lambda j: (B.x_ready.sem, B.x_ready.count(it, T_ATT * PAIRS + j + 1)),
                          lambda j: turn(it, B, h3[:, j, :, :], B, LN_FFN, j, (B.v_copied, j) if j else None), tick)
                moe(it, tick)

            run(pe, half_a, half_b)

        @block.scalar
        def _(act):
            def copy_x(it, st, stage, j, dst):
                act.wait_ge(st.turned.sem, st.turned.count(it, stage * PAIRS + j + 1))
                for h in range(2):
                    half = act.copy(dst[0:FEAT, 2 * j:2 * j + 2, h * HALF:(h + 1) * HALF],
                                    st.bank_g[h * FEAT:(h + 1) * FEAT, 0:TOKENS].rearrange("p (b s) -> p b s", b=2))
                half.then_inc(st.x_ready.sem, 1)

            def square(it, st, ln, j):
                act.wait_ge(st.centred[ln].sem, st.centred[ln].count(it, j + 1))
                act.activation(st.sq[:, j, :, :], st.cen[:, j, :, :], ACT.Square).then_inc(st.squared[ln].sem, 1)

            def attention(name, it, st, layer, stage, first_ln, biases, tick):
                def copy_g(j):
                    n = layer * PAIRS + j
                    act.wait_ge(st.g_ready.sem, st.g_ready.count(it, n + 1))
                    act.copy(st.gT[:, j % 2, :], st.bank_g[:, :]).then_inc(st.g_copied.sem, 1)

                def copy_v(j):
                    n = layer * PAIRS + j
                    act.wait_ge(st.v_ready.sem, st.v_ready.count(it, n + 1))
                    act.copy(st.val[0:HALF, j, :, :], st.bank_g[0:HALF, 0:4 * AUG].rearrange("p (t e) -> p t e", t=4))\
                       .then_inc(st.v_copied.sem, 1)

                def exponent(k):
                    act.wait_ge(st.peaked.sem, st.peaked.count(it, layer * GROUP + k + 1))
                    for h in range(2):
                        scores = st.prob[:, k % 4, h, :] if biases else st.bank_s[0:HALF, h * TOKENS:(h + 1) * TOKENS]
                        exp = act.activation(st.prob[:, k % 4, h, :], scores, ACT.Exp, bias=st.peak[:, k % 4, h:h + 1])
                    exp.then_inc(st.exp_done.sem, 1)

                def copy_probs(k):
                    act.wait_ge(st.probs_turned.sem, st.probs_turned.count(it, layer * GROUP + k + 1))
                    act.copy(st.probT[0:HALF, k % 2, :, :], st.bank_p[0:HALF, :].rearrange("p (h s) -> p h s", h=2))\
                       .then_inc(st.probT_ready.sem, 1)

                if (k := due(name + ".exp", tick)) is not None:
                    exponent(k)
                if (k := due(name + ".copy_probs", tick)) is not None:
                    copy_probs(k)
                if (j := due(name + ".square", tick)) is not None:
                    square(it, st, first_ln, j)
                if (j := due(name + ".copy_v", tick)) is not None:
                    copy_v(j)
                if (j := due(name + ".copy_g", tick)) is not None:
                    copy_g(j)
                if stage is not None and (j := due(name + ".copy_x", tick)) is not None:
                    copy_x(it, st, stage, j, st.xT)

            def ffn(it, tick):
                if (j := due("ffn.gelu", tick)) is not None:
                    for c in range(2):
                        act.wait_ge(hid_ready.sem, hid_ready.count(it, 2 * j + c + 1))
                        act.activation(hid[:, j % 2, c, :], B.bank[c][:, :], ACT.Gelu_apprx_tanh).then_inc(gelu_done.sem, 1)
                if (j := due("ffn.copy_y", tick)) is not None:
                    act.wait_ge(B.out_ready.sem, B.out_ready.count(it, O_FFN * PAIRS + j + 1))
                    act.copy(pairwise(y[:, j, :, :]), B.outputs(FEAT)).then_inc(B.out_read.sem, 1)
                if (j := due("ffn.square", tick)) is not None:
                    square(it, B, LN_FFN, j)

            def moe(it, tick):
                if (j := due("moe.copy_hot", tick)) is not None:
                    act.wait_ge(hot_turned.sem, hot_turned.count(it, j + 1))
                    act.copy(B.xT[HOT:ROWS, 2 * j:2 * j + 2, :], B.bank_g[0:EXPERTS, :].rearrange("p (b s) -> p b s", b=2))\
                       .then_inc(hot_ready.sem, 1)
                for half in range(2):
                    if (j := due(("moe.relu01", "moe.relu23")[half], tick)) is not None:
                        act.wait_ge(ehid_ready.sem, ehid_ready.count(it, 4 * j + 2 * half + 1))
                        act.activation(ehid[:, j % 2, 2 * half, :], B.bank[0][:, :], ACT.Relu).then_inc(relu_act.sem, 1)
                if (j := due("moe.copy_x", tick)) is not None:
                    copy_x(it, B, T_MOE, j, B.xT)
                if (j := due("moe.square", tick)) is not None:
                    square(it, B, LN_MOE, j)

            def half_a(it, tick):
                if due("conv.bias", tick) is not None:
                    for c in range(CHANNELS):
                        on = slice((c % 2) * FEAT, (c % 2 + 1) * FEAT)
                        act.wait_ge(conv_ready.sem, conv_ready.count(it, c // 2 + 1))
                        act.activation(featT[0:FEAT, :, c * PER_CHANNEL:(c + 1) * PER_CHANNEL],
                                       A.bank[c // 2][on, :].rearrange("p (b j) -> p b j", b=GROUP),
                                       ACT.Identity, bias=P("convb", c, c + 1)[on, :]).then_inc(feat_ready.sem, 1)
                attention("att0", it, A, 0, None, LN_IN, False, tick)
                attention("att1", it, A, 1, 0, LN_ATT, True, tick)
                if (j := due("router.square", tick)) is not None:
                    square(it, A, LN_B, j)
                if (j := due("router.copy_x", tick)) is not None:
                    copy_x(it, A, T_FFN, j, h2T)

            def half_b(it, tick):
                ffn(it, tick)
                attention("att2", it, B, 0, T_ATT, LN_D, False, tick)
                moe(it, tick)

            act.wait_ge(conv_params_in.sem, 16)
            act.activation(first_exp[:, :], P("convb", 0, 1)[0:FEAT, :], ACT.Exp)
            run(act, half_a, half_b)

        @block.vector
        def _(dve):
            dve.memset(neg_half[:, :], -0.5)
            dve.wait_ge(conv_params_in.sem, 16)
            for c in range(CHANNELS):
                for a in range(2):
                    dve.tensor_scalar(conv_lhs[:, c // 2, a, (c % 2) * FEAT:(c % 2 + 1) * FEAT], P("eye2"), P("convw", 2 * c + a, 2 * c + a + 1), None, ALU.mult)
            dve.tensor_copy(featT[:, :, :], row(P("xinit"), GROUP)).then_inc(conv_set.sem, 1)
            dve.wait_ge(fold_params_in.sem, 16)
            qkv_cols = par[0:FEAT, START["wqB"]:START["wqB"] + 3 * FEAT].rearrange("p (n c) -> p n c", n=3)
            dve.tensor_tensor(fold_tmp[:, :, :], qkv_cols, row(P("b1"), 3), ALU.mult).then_inc(folded_dve.sem, 1)
            dve.wait_ge(folded_dve.sem, 1)
            dve.tensor_reduce(qkv_sum[:, :], fold_tmp[:, :, :], AX_X, ALU.add).then_inc(folded_dve.sem, 1)
            dve.wait_ge(folded_dve.sem, 2)
            dve.tensor_tensor(qkv_fold[:, :, 0:FEAT], qkv_cols, row(P("g1"), 3), ALU.mult)
            dve.memset(qkv_fold[:, :, AUG:ROWS], 0.0)
            dve.tensor_tensor(qkv_fold[:, :, FEAT:AUG], qkv_sum[:, :].unsqueeze(2), P("qkvb").unsqueeze(2), ALU.add)\
               .then_inc(folded_dve.sem, 1)
            root = 1.0 / float(FEAT) ** 0.5
            dve.wait_ge(folded_pe.sem, 1)
            dve.tensor_scalar(a_mat[0][:, :], B.bank[0][:, 0:ROWS], root, None, ALU.mult)
            dve.scalar_tensor_tensor(a_mat[2][:, :], B.bank[1][:, 0:ROWS], root, P("betaD"), ALU.mult, ALU.add)
            dve.tensor_copy(v_mat[0][:, FEAT:AUG], P("vaddA", FEAT, AUG))
            dve.tensor_tensor(v_mat[0][:, 0:FEAT], B.bank[2][:, 0:FEAT], P("vaddA", 0, FEAT), ALU.add)
            dve.wait_ge(folded_pe.sem, 2)
            for t in (A.xT, B.xT, h2T):
                dve.tensor_copy(t[:, :, :], row(P("xinit"), GROUP))
            dve.tensor_copy(a_mat[1][:, :], B.bank[3][:, 0:ROWS])
            dve.tensor_copy(v_mat[1][:, FEAT:AUG], P("vaddB", FEAT, AUG))
            dve.scalar_tensor_tensor(v_mat[1][:, 0:FEAT], B.bank[3][:, ROWS:ROWS + FEAT], P("scaleB"),
                                     P("vaddB", 0, FEAT), ALU.mult, ALU.add).then_inc(setup_done.sem, 1)

            def centre(it, st, ln, j, src, sem, need):
                n = ln * PAIRS + j
                dve.wait_ge(sem, need)
                dve.tensor_reduce(st.mean[:, j, :], src, AX_X, ALU.add).then_inc(st.summed[ln].sem, 1)
                dve.wait_ge(st.summed[ln].sem, st.summed[ln].count(it, j + 1))
                dve.scalar_tensor_tensor(st.cen[:, j, :, :], bc(st.mean[:, j, :], FEAT), -1.0 / FEAT, src,
                                         ALU.mult, ALU.add).then_inc(st.centred[ln].sem, 1)

            def variance(it, st, ln, j):
                dve.wait_ge(st.squared[ln].sem, st.squared[ln].count(it, j + 1))
                dve.tensor_reduce(st.var[:, j, :], st.sq[:, j, :, :], AX_X, ALU.add).then_inc(st.var_ready[ln].sem, 1)

            def attention(name, it, st, layer, out_at, first_ln, biases, dst, tick):
                def find_peak(k):
                    n = layer * GROUP + k
                    s = st.bank_s[0:HALF, :].rearrange("p (h t) -> p h t", h=2)
                    prob = st.prob[:, k % 4, :, :]
                    dve.wait_ge(st.scores_ready.sem, st.scores_ready.count(it, n + 1))
                    if biases:
                        dve.tensor_tensor(prob, s, P("bias").rearrange("p (h t) -> p h t", h=2), ALU.add)\
                           .then_inc(biased.sem, 1)
                        dve.wait_ge(biased.sem, biased.count(it, k + 1))
                        s = prob
                    dve.tensor_reduce(st.peak[:, k % 4, :], s, AX_X, ALU.max, negate=True).then_inc(st.peaked.sem, 1)

                def divide(j):
                    n = layer * PAIRS + j
                    o = st.outputs(AUG)
                    sums = st.rsum[:, j, :].rearrange("p (b h) -> p b h", b=2)
                    dve.wait_ge(st.out_ready.sem, st.out_ready.count(it, out_at * PAIRS + j + 1))
                    dve.reciprocal(sums, o[:, :, :, FEAT]).then_inc(st.sum_inverted.sem, 1)
                    dve.wait_ge(st.sum_inverted.sem, st.sum_inverted.count(it, n + 1))
                    dve.tensor_tensor(pairwise(dst[:, j, :, :]), o[:, :, :, 0:FEAT],
                                      sums.unsqueeze(3).to_broadcast([HALF, 2, 2, FEAT]), ALU.mult)\
                       .then_inc(st.out_read.sem, 1)

                def centre_output(j):
                    done = st.out_read.count(it, out_at * PAIRS + j + 1)
                    if dst is not B.u:
                        centre(it, st, first_ln, j, dst[:, j, :, :], st.out_read.sem, done)
                    else:
                        dve.wait_ge(st.out_read.sem, done)
                        dve.tensor_tensor(B.u[:, j, :, :], B.u[:, j, :, :], h3[:, j, :, :], ALU.add).then_inc(att_ready.sem, 1)
                        centre(it, st, first_ln, j, B.u[:, j, :, :], att_ready.sem, att_ready.count(it, j + 1))

                if (k := due(name + ".peak", tick)) is not None:
                    find_peak(k)
                if (j := due(name + ".divide", tick)) is not None:
                    divide(j)
                if (j := due(name + ".centre", tick)) is not None:
                    centre_output(j)
                if (j := due(name + ".variance", tick)) is not None:
                    variance(it, st, first_ln, j)

            def then_top(it, n, ins):
                ins.then_inc(top_step.sem, 1)
                dve.wait_ge(top_step.sem, top_step.count(it, n + 1))
                hold(dve, dve_gate)

            def ffn(it, tick):
                def round_of_8(r):
                    then_top(it, 2 * r + 1, dve.max(top8[:, :], work[:, :]))
                    then_top(it, 2 * r + 2, dve.match_replace(work[:, :], top8[:, :], work[:, :], LOWEST))

                rounds = TOPK // 8
                if due("ffn.top_start", tick) is not None:
                    dve.wait_ge(w_turned.sem, w_turned.count(it, 1))
                    dve.tensor_copy(work[:, :], B.bank_g[0:GROUP, 32:32 + TOKENS])
                    then_top(it, 0, dve.tensor_copy(wrow[:, :], B.bank_g[0:GROUP, 32:32 + TOKENS]))
                if (r := due("ffn.top_round", tick)) is not None and r < rounds:
                    round_of_8(r)
                if due("ffn.top_end", tick) is not None:
                    n = 2 * (TOPK // 8) + 1
                    then_top(it, n, dve.max(top8[:, :], work[:, :]))
                    then_top(it, n + 1, dve.memset(top8[:, TOPK % 8:8], LOWEST))
                    then_top(it, n + 2, dve.match_replace(work[:, :], top8[:, :], work[:, :], LOWEST))
                    then_top(it, n + 3, dve.tensor_tensor(work[:, :], work[:, :], wrow[:, :], ALU.not_equal))
                    then_top(it, n + 4, dve.tensor_tensor(wmrow[:, :], work[:, :], wrow[:, :], ALU.mult))
                if due("ffn.copy_wm", tick) is not None:
                    dve.wait_ge(wm_turned.sem, wm_turned.count(it, 1))
                    dve.tensor_copy(wm[:, :, :], B.bank_g[0:HALF, 192:192 + 2 * GROUP].rearrange("p (h b) -> p h b", h=2))\
                       .then_inc(wm_ready.sem, 1)
                if (j := due("ffn.centre", tick)) is not None:
                    dve.wait_ge(y_scaled.sem, y_scaled.count(it, j + 1))
                    dve.scalar_tensor_tensor(B.u[:, j, :, :], h2[:, j, :, :], 2.0, y[:, j, :, :], ALU.mult, ALU.add)\
                       .then_inc(u_ready.sem, 1)
                    centre(it, B, LN_FFN, j, B.u[:, j, :, :], u_ready.sem, u_ready.count(it, j + 1))
                if (j := due("ffn.variance", tick)) is not None:
                    variance(it, B, LN_FFN, j)

            def moe(it, tick):
                def pick(j):
                    lg = B.bank_g[0:HALF, 0:4 * EXPERTS].rearrange("p (t e) -> p t e", t=4)
                    dve.wait_ge(logits_ready.sem, logits_ready.count(it, j + 1))
                    dve.tensor_reduce(lmax[:, j, 0, :], lg, AX_X, ALU.max).then_inc(route.sem, 1)
                    dve.wait_ge(route.sem, route.count(it, 4 * j + 1))
                    dve.tensor_tensor(hit[:, j, :, :], lg, bc(lmax[:, j, 0, :], EXPERTS), ALU.is_equal).then_inc(route.sem, 1)
                    dve.wait_ge(route.sem, route.count(it, 4 * j + 2))
                    dve.tensor_tensor(rank[:, j, :, :], hit[:, j, :, :], row(P("desc"), 4), ALU.mult).then_inc(route.sem, 1)
                    dve.wait_ge(route.sem, route.count(it, 4 * j + 3))
                    dve.tensor_reduce(lmax[:, j, 1, :], rank[:, j, :, :], AX_X, ALU.max).then_inc(route.sem, 1)
                    dve.wait_ge(route.sem, route.count(it, 4 * j + 4))
                    dve.tensor_tensor(one_hot[:, j, :, :], rank[:, j, :, :], bc(lmax[:, j, 1, :], EXPERTS), ALU.is_equal)\
                       .then_inc(routed.sem, 1)

                if (j := due("moe.pick", tick)) is not None:
                    pick(j)
                for half in range(2):
                    if (j := due(("moe.relu01", "moe.relu23")[half], tick)) is not None:
                        dve.wait_ge(ehid_ready.sem, ehid_ready.count(it, 4 * j + 2 * half + 2))
                        dve.tensor_scalar(ehid[:, j % 2, 2 * half + 1, :], B.bank[1][:, :], 0.0, None, ALU.max)\
                           .then_inc(relu_dve.sem, 1)
                if (j := due("moe.centre", tick)) is not None:
                    dve.wait_ge(B.out_ready.sem, B.out_ready.count(it, O_MOE * PAIRS + j + 1))
                    dve.scalar_tensor_tensor(pairwise(B.u[:, j, :, :]), B.outputs(FEAT), 0.0,
                                             pairwise(feat_d[:, j, :, :]), ALU.max, ALU.add).then_inc(B.out_read.sem, 1)
                    centre(it, B, LN_MOE, j, B.u[:, j, :, :], B.out_read.sem, B.out_read.count(it, O_MOE * PAIRS + j + 1))
                if (j := due("moe.variance", tick)) is not None:
                    variance(it, B, LN_MOE, j)

            def half_a(it, tick):
                attention("att0", it, A, 0, 0, LN_IN, False, h1, tick)
                attention("att1", it, A, 1, 1, LN_ATT, True, att, tick)
                if (j := due("router.gain", tick)) is not None:
                    dve.wait_ge(A.normed[LN_ATT].sem, A.normed[LN_ATT].count(it, j + 1))
                    dve.tensor_tensor(on[:, j, :, :], on[:, j, :, :], row(P("g2"), 4), ALU.mult).then_inc(gained.sem, 1)
                    dve.wait_ge(gained.sem, gained.count(it, 2 * j + 1))
                    dve.wait_ge(res_ready.sem, res_ready.count(it, j + 1))
                    dve.tensor_tensor(A.u[:, j, :, :], on[:, j, :, :], resid[:, j, :, :], ALU.add).then_inc(gained.sem, 1)
                if (j := due("router.centre", tick)) is not None:
                    centre(it, A, LN_B, j, A.u[:, j, :, :], gained.sem, gained.count(it, 2 * j + 2))
                if (j := due("router.variance", tick)) is not None:
                    variance(it, A, LN_B, j)
                if due("router.copy_w", tick) is not None:
                    dve.wait_ge(w_ready.sem, w_ready.count(it, 1))
                    dve.tensor_copy(wcol[:, :, :], A.bank_o[0:HALF, 0:2 * GROUP].rearrange("p (h b) -> p h b", h=2))\
                       .then_inc(w_copied.sem, 1)

            def half_b(it, tick):
                ffn(it, tick)
                attention("att2", it, B, 0, O_ATT, LN_D, False, B.u, tick)
                moe(it, tick)

            run(dve, half_a, half_b)

        @block.gpsimd
        def _(pool):
            for last in stored:
                pool.sem_inc(last.sem, last.head)
            for t in (A.probT, B.probT, A.val, B.val):
                fill = pool.memset(t[:], 0.0)
            fill.then_inc(padded.sem, 1)
            pool.wait_ge(layer_params_in.sem, 16)
            pool.wait_ge(setup_done.sem, 1)

            def scale(it, st, ln, j, dst):
                n = ln * PAIRS + j
                pool.wait_ge(st.var_ready[ln].sem, st.var_ready[ln].count(it, j + 1))
                hold(pool, pool_gate)
                pool.tensor_scalar(st.rstd[:, j, :], st.var[:, j, :], 1.0 / FEAT, EPS, ALU.mult, ALU.add)\
                    .then_inc(st.var_eps[ln].sem, 1)
                pool.wait_ge(st.var_eps[ln].sem, st.var_eps[ln].count(it, j + 1))
                pool.tensor_tensor(st.rstd[:, j, :], st.rstd[:, j, :], neg_half[:, :], ALU.pow).then_inc(st.rstd_ready[ln].sem, 1)
                pool.wait_ge(st.rstd_ready[ln].sem, st.rstd_ready[ln].count(it, j + 1))
                pool.tensor_tensor(dst, st.cen[:, j, :, :], bc(st.rstd[:, j, :], FEAT), ALU.mult).then_inc(st.normed[ln].sem, 1)

            def half_a(it, tick):
                if (j := due("att0.norm", tick)) is not None:
                    scale(it, A, LN_IN, j, xn[:, j, :, :])
                    pool.tensor_tensor(resid[:, j, :, :], h1[:, j, :, :], row(P("b2"), 4), ALU.add).then_inc(res_ready.sem, 1)
                if (j := due("att1.norm", tick)) is not None:
                    scale(it, A, LN_ATT, j, on[:, j, :, :])
                if (j := due("router.norm", tick)) is not None:
                    if it.ahead:
                        pool.wait_ge(u_ready.sem, u_ready.count(When(it.reg, it.ahead - 1), j + 1))
                    scale(it, A, LN_B, j, h2[:, j, :, :])

            def half_b(it, tick):
                if (j := due("ffn.bias", tick)) is not None:
                    pool.wait_ge(B.out_read.sem, B.out_read.count(it, O_FFN * PAIRS + j + 1))
                    pool.tensor_tensor(y[:, j, :, :], y[:, j, :, :], row(P("fb2"), 4), ALU.add).then_inc(y_biased.sem, 1)
                if (j := due("ffn.weight", tick)) is not None:
                    if j == 0:
                        pool.wait_ge(wm_ready.sem, wm_ready.count(it, 1))
                    pool.wait_ge(y_biased.sem, y_biased.count(it, j + 1))
                    w = wm[:, :, 2 * j:2 * j + 2].rearrange("p h b -> p b h").unsqueeze(3).to_broadcast([HALF, 2, 2, FEAT])
                    pool.tensor_tensor(pairwise(y[:, j, :, :]), pairwise(y[:, j, :, :]), w, ALU.mult).then_inc(y_scaled.sem, 1)
                if (j := due("ffn.norm", tick)) is not None:
                    scale(it, B, LN_FFN, j, h3[:, j, :, :])
                if (j := due("att2.norm", tick)) is not None:
                    scale(it, B, LN_D, j, feat_d[:, j, :, :])
                if (j := due("moe.norm", tick)) is not None:
                    pool.wait_ge(stored[j].sem, stored[j].count(it, 0))
                    scale(it, B, LN_MOE, j, res[:, j, :, :])

            run(pool, half_a, half_b)


def _lay_out(inputs):
    f = {k: np.ascontiguousarray(np.asarray(v), dtype=np.float32) for k, v in inputs.items()}
    x = f["x"].reshape(IMAGES, 48, 2, 48, 2).transpose(2, 4, 0, 1, 3)
    x = x.reshape(2, 2, IMAGES, PER_CHANNEL, FEAT).transpose(1, 4, 0, 2, 3)
    pixels = np.ascontiguousarray(x).reshape(2 * FEAT, 2, IMAGES, PER_CHANNEL)

    par = np.zeros((128, PARAM_COLS), np.float32)

    def put(name, array, row=0, col=0):
        a = np.asarray(array, np.float32)
        c = START[name] + col
        par[row:row + a.shape[0], c:c + a.shape[1]] = a

    def rep(vector, rows):
        return np.broadcast_to(vector.reshape(1, -1), (rows, vector.size))

    put("ident", np.eye(128))
    put("eye2", np.eye(FEAT))
    put("eye2", np.eye(FEAT), row=FEAT)
    cw = f["L0_tok_conv_w"].reshape(CHANNELS, 2, 2)
    for b in range(2):
        put("convw", rep(cw[:, :, b], FEAT), row=b * FEAT)
    put("convb", rep(f["L0_tok_conv_b"], 128))
    pos = np.arange(TOKENS, dtype=np.float64)
    put("xinit", np.ones((1, TOKENS)), row=ONE)
    for n, period in enumerate(SCALES):
        put("xinit", np.stack([np.cos(2 * np.pi * pos / period), np.sin(2 * np.pi * pos / period)]), row=AUG + 2 * n)
    for name, w, b in (("wqA", "L0_tok_wq", "L0_tok_bq"), ("wkA", "L0_tok_wk", "L0_tok_bk"), ("wvA", "L0_tok_wv", "L0_tok_bv"),
                       ("wqD", "L1_attn_Wq", "L1_attn_bq"), ("wkD", "L1_attn_Wk", "L1_attn_bk")):
        put(name, f[w])
        put(name, f[b][:, None], col=FEAT)
    put("woA", f["L0_tok_wo"].T)
    put("vaddA", f["L0_tok_bo"][None], row=ONE)
    put("vaddA", np.ones((1, 1)), row=ONE, col=FEAT)
    qkv = f["L0_attn_qkv_w"].T
    for n, name in enumerate(("wqB", "wkB", "wvB")):
        put(name, qkv[n * FEAT:(n + 1) * FEAT])
        put("qkvb", f["L0_attn_qkv_b"][n * FEAT:(n + 1) * FEAT, None], col=n)
    put("g1", rep(f["L0_attn_ln1_g"], FEAT))
    put("b1", rep(f["L0_attn_ln1_b"], FEAT))
    put("projB", f["L0_attn_proj_w"])
    put("scaleB", rep(f["L0_attn_scale"].reshape(1), 128))
    put("vaddB", f["L0_attn_proj_b"][None], row=ONE)
    put("vaddB", np.ones((1, 1)), row=ONE, col=FEAT)
    put("g2", rep(f["L0_attn_ln2_g"], HALF))
    put("b2", rep(f["L0_attn_ln2_b"], HALF))
    table = f["L0_attn_bias_table"]
    key = np.arange(TOKENS)
    for h in range(2):
        query = h * HALF + np.arange(HALF)
        put("bias", table[key[None, :] - query[:, None] + TOKENS - 1], col=h * TOKENS)
    put("wr", f["L0_ffn_wr"])
    put("wr", f["L0_ffn_br"][None], row=ONE)
    put("w1", f["L0_ffn_w1"])
    put("w1", f["L0_ffn_b1"][None], row=ONE)
    for c in range(2):
        put("w2", f["L0_ffn_w2"][c * 128:(c + 1) * 128], col=c * FEAT)
    put("fb2", rep(f["L0_ffn_b2"], HALF))
    for n in range(2):
        for r in range(2):
            put("betaD", f["L1_attn_beta"][n].reshape(1, 1), row=AUG + 2 * n + r, col=AUG + 2 * n + r)
    put("vD", f["L1_attn_Wv"].T)
    put("vD", f["L1_attn_bv"][None], row=ONE)
    put("vD", np.ones((1, 1)), row=ONE, col=FEAT)
    put("router", f["L1_ffn_router_w"].T)
    put("router", f["L1_ffn_router_b"][None], row=ONE)
    put("ew1", f["L1_ffn_W1"].transpose(1, 0, 2).reshape(FEAT, MOE_H))
    put("ew1", np.full((EXPERTS, MOE_H), OFF), row=HOT)
    for e in range(EXPERTS):
        put("ew1", f["L1_ffn_b1"][e][None], row=HOT + e, col=e * HIDDEN)
    w2 = f["L1_ffn_W2"].reshape(MOE_H, FEAT)
    for c in range(4):
        put("ew2", w2[c * 128:(c + 1) * 128], col=c * FEAT)
    put("eb2", f["L1_ffn_b2"], row=HOT)
    put("desc", rep(np.arange(EXPERTS, 0, -1), HALF))
    return pixels, par


def kernel(**inputs):
    import concourse.bacc as bacc
    from concourse.bass_utils import run_bass_kernel_spmd

    pixels, par = _lay_out(inputs)
    nc = bacc.Bacc("TRN2", target_bir_lowering=False, num_devices=1)
    pixels_dram = nc.dram_tensor("pixels", pixels.shape, F32, kind="ExternalInput").ap()
    params_dram = nc.dram_tensor("params", par.shape, F32, kind="ExternalInput").ap()
    out_dram = nc.dram_tensor("out", (IMAGES, TOKENS, FEAT), F32, kind="ExternalOutput").ap()
    build(nc, pixels_dram, params_dram, out_dram)
    r = run_bass_kernel_spmd(nc, [{"pixels": pixels, "params": par}], core_ids=[0])
    return r.results[0]["out"]
```
